# Optimizing a Trainium2 kernel written in Bass

```python
import numpy as np
import jax
import jax.numpy as jnp

def _softmax(x, axis=-1):
    return jax.nn.softmax(x, axis=axis)

def _gelu(x):
    return jax.nn.gelu(x, approximate=True)

def _silu(x):
    return jax.nn.silu(x)

def _sigmoid(x):
    return jax.nn.sigmoid(x)

def _layernorm(x, axis=-1, eps=1e-05):
    m = jnp.mean(x, axis=axis, keepdims=True)
    v = jnp.var(x, axis=axis, keepdims=True)
    return (x - m) / jnp.sqrt(v + eps)

def _scatter_add(tgt, idx, src, axis=0):
    return tgt.at[idx].add(src)

def _segment_sum(src, seg, n):
    return jax.ops.segment_sum(src, seg, n)
kernel_name = 'mk_adj_resnorm_d2_adj_r2_f4ddbf'

def setup_inputs(seed: int=0):
    np.random.seed(seed)
    _w = jnp.asarray

    def _rec_inputs():
        import jax
        import jax.numpy as jnp
        _gk = jax.random.key(seed)
        x = -0.000125 + 0.9999 * jax.random.normal(jax.random.fold_in(_gk, 1), (128, 128, 128), jnp.float32)
        _a = jax.random.bernoulli(jax.random.fold_in(_gk, 2), 0.0625, (128, 128))
        _a = jnp.logical_or(_a, jnp.swapaxes(_a, -1, -2))
        _a = jnp.logical_or(_a, jnp.eye(128, dtype=bool))
        _af = _a.astype(jnp.float32)
        _af = _af * jax.random.uniform(jax.random.fold_in(_gk, 3), (128, 128), jnp.float32, 0.05, 0.000488281)
        adj = _af
        return (x, adj)
    x, adj = _rec_inputs()

    def _L0_gnn_setup():
        import jax, jax.numpy as jnp
        import numpy as np
        B, T, D, H = (64, 1024, 128, 128)
        MAX_SKIP = 4

        def _lstm_last(Wih, Whh, bih, bhh, xs):
            N, _, Hd = xs.shape
            bias = bih + bhh

            def step(carry, x_t):
                h, c = carry
                g = x_t @ Wih.T + h @ Whh.T + bias
                i, f, gg, o = jnp.split(g, 4, axis=-1)
                c = jax.nn.sigmoid(f) * c + jax.nn.sigmoid(i) * jnp.tanh(gg)
                h = jax.nn.sigmoid(o) * jnp.tanh(c)
                return ((h, c), None)
            init = (jnp.zeros((N, Hd), xs.dtype), jnp.zeros((N, Hd), xs.dtype))
            (h_last, _), _ = jax.lax.scan(step, init, jnp.swapaxes(xs, 0, 1))
            return h_last
        key = jax.random.key(seed)
        ks = jax.random.split(key, 8)
        s = 0.05
        x = jax.random.normal(ks[0], (B, T, D), jnp.float32)
        adj = jax.random.uniform(ks[1], (T, T), jnp.float32) / T
        Wg0 = jax.random.normal(ks[2], (D, H), jnp.float32) * s
        bg0 = jnp.zeros((H,), jnp.float32)
        Wg1 = jax.random.normal(ks[3], (H, H), jnp.float32) * s
        bg1 = jnp.zeros((H,), jnp.float32)
        Wih = jax.random.normal(ks[4], (MAX_SKIP, 4 * H, H), jnp.float32) * s
        Whh = jax.random.normal(ks[5], (MAX_SKIP, 4 * H, H), jnp.float32) * s
        bih = jax.random.normal(ks[6], (MAX_SKIP, 4 * H), jnp.float32) * s
        bhh = jax.random.normal(ks[7], (MAX_SKIP, 4 * H), jnp.float32) * s
        return dict(x=x, adj=adj, Wg0=Wg0, bg0=bg0, Wg1=Wg1, bg1=bg1, Wih=Wih, Whh=Whh, bih=bih, bhh=bhh)
    _L0_gnn_all = _L0_gnn_setup()
    _L0_gnn_in = {k: v for k, v in _L0_gnn_all.items() if k in ('Wg0', 'bg0', 'Wg1', 'bg1', 'Wih', 'Whh', 'bih', 'bhh')}
    del _L0_gnn_all

    def _L1_gnn_setup():
        import jax, jax.numpy as jnp
        import numpy as np
        B, N, IN_DIM, OUT_DIM, H = (2, 2048, 128, 128, 4)
        HEAD_DIM = OUT_DIM // H
        EDGE_P = 0.01
        key = jax.random.key(seed)
        k1, k2, k3 = jax.random.split(key, 3)
        h = jax.random.normal(k1, (B, N, IN_DIM), dtype=jnp.float32)
        W = jax.random.normal(k2, (IN_DIM, 3 * OUT_DIM), dtype=jnp.float32) / np.sqrt(IN_DIM)
        adj = (jax.random.uniform(k3, (N, N)) < EDGE_P).astype(jnp.float32)
        adj = jnp.maximum(adj, jnp.eye(N, dtype=jnp.float32))
        return {'h': h, 'W': W, 'adj': adj}
    _L1_gnn_all = _L1_gnn_setup()
    _L1_gnn_in = {k: v for k, v in _L1_gnn_all.items() if k in ('W',)}
    del _L1_gnn_all
    return {'x': x, 'adj': adj, 'L0_gnn_Wg0': _L0_gnn_in['Wg0'], 'L0_gnn_bg0': _L0_gnn_in['bg0'], 'L0_gnn_Wg1': _L0_gnn_in['Wg1'], 'L0_gnn_bg1': _L0_gnn_in['bg1'], 'L0_gnn_Wih': _L0_gnn_in['Wih'], 'L0_gnn_Whh': _L0_gnn_in['Whh'], 'L0_gnn_bih': _L0_gnn_in['bih'], 'L0_gnn_bhh': _L0_gnn_in['bhh'], 'L1_gnn_W': _L1_gnn_in['W']}

def reference(x, adj, L0_gnn_Wg0, L0_gnn_bg0, L0_gnn_Wg1, L0_gnn_bg1, L0_gnn_Wih, L0_gnn_Whh, L0_gnn_bih, L0_gnn_bhh, L1_gnn_W):
    import jax
    import jax.numpy as jnp

    def _L0_gnn_ref(x, adj, Wg0, bg0, Wg1, bg1, Wih, Whh, bih, bhh):
        import jax, jax.numpy as jnp
        import numpy as np
        B, T, D, H = (64, 1024, 128, 128)
        MAX_SKIP = 4

        def _lstm_last(Wih, Whh, bih, bhh, xs):
            N, _, Hd = xs.shape
            bias = bih + bhh

            def step(carry, x_t):
                h, c = carry
                g = x_t @ Wih.T + h @ Whh.T + bias
                i, f, gg, o = jnp.split(g, 4, axis=-1)
                c = jax.nn.sigmoid(f) * c + jax.nn.sigmoid(i) * jnp.tanh(gg)
                h = jax.nn.sigmoid(o) * jnp.tanh(c)
                return ((h, c), None)
            init = (jnp.zeros((N, Hd), xs.dtype), jnp.zeros((N, Hd), xs.dtype))
            (h_last, _), _ = jax.lax.scan(step, init, jnp.swapaxes(xs, 0, 1))
            return h_last
        h = jax.nn.relu(jnp.einsum('ts,bsh->bth', adj, x @ Wg0 + bg0))
        h = jax.nn.relu(jnp.einsum('ts,bsh->bth', adj, h @ Wg1 + bg1))
        Bv, Tv, Hd = h.shape
        for p in range(1, MAX_SKIP + 1):
            nw = Tv // p
            wins = h[:, :nw * p, :].reshape(Bv * nw, p, Hd)
            last = _lstm_last(Wih[p - 1], Whh[p - 1], bih[p - 1], bhh[p - 1], wins)
            idx = jnp.arange(nw) * p + (p - 1)
            h = h.at[:, idx, :].set(last.reshape(Bv, nw, Hd))
        return h

    def _L1_gnn_ref(h, W, adj):
        import jax, jax.numpy as jnp
        import numpy as np
        B, N, IN_DIM, OUT_DIM, H = (2, 2048, 128, 128, 4)
        HEAD_DIM = OUT_DIM // H
        EDGE_P = 0.01
        Bn, Nn, _ = h.shape
        qkv = h @ W
        qkv = qkv.reshape(Bn, Nn, 3, H, HEAD_DIM).transpose(2, 0, 3, 1, 4)
        q, k, v = (qkv[0], qkv[1], qkv[2])
        mask = jnp.where(adj == 0, -jnp.inf, 0.0)
        scores = jnp.einsum('bhid,bhjd->bhij', q, k) / np.sqrt(HEAD_DIM) + mask
        attn = jax.nn.softmax(scores, axis=-1)
        out = jnp.einsum('bhij,bhjd->bhid', attn, v)
        return out.transpose(0, 2, 1, 3).reshape(Bn, Nn, OUT_DIM)
    x = _layernorm(x + _L0_gnn_ref(x, adj, L0_gnn_Wg0, L0_gnn_bg0, L0_gnn_Wg1, L0_gnn_bg1, L0_gnn_Wih, L0_gnn_Whh, L0_gnn_bih, L0_gnn_bhh), axis=-1)
    x = _layernorm(x + _L1_gnn_ref(x, L1_gnn_W, adj), axis=-1)
    return x

_drawn_inputs = setup_inputs


def setup_inputs(seed=0):
    import zlib

    import numpy as np

    out = dict(_drawn_inputs(seed))
    spreads = {'L0_gnn_bg0': (0.0, 0.8), 'L0_gnn_bg1': (0.0, 0.8)}
    factors = {'L0_gnn_Wg0': 8.0, 'L0_gnn_Wg1': 8.0, 'L0_gnn_Wih': 7.589, 'L0_gnn_Whh': 8.0}
    for name, (base, spread) in spreads.items():
        noise = np.random.default_rng([zlib.crc32(name.encode()), seed]).standard_normal(out[name].shape)
        drawn = base * np.exp(spread * noise) if base else spread * noise
        out[name] = jnp.asarray(drawn.astype(out[name].dtype))
    for name, factor in factors.items():
        out[name] = (out[name] * factor).astype(out[name].dtype)
    return out
```

```python
from contextlib import ExitStack

import numpy as np

import concourse.bass as bass
from concourse import mybir

F32 = mybir.dt.float32
F16 = mybir.dt.float16
BF16 = mybir.dt.bfloat16
ALU = mybir.AluOpType
ACT = mybir.ActivationFunctionType
AX_X = mybir.AxisListType.X

P = 128
B, T, D = 128, 128, 128
GB = 8
QB = 4
NQ = GB // QB
NG = B // GB
W = QB * T
HEADS, HD = 4, 32
MAX_SKIP = 4
EPS = 1e-5
MASKED = -1e30
VW = HD + 1
VSPAN = 3 * VW
VSTEP = 4 * VW
I_, F_, G_, O_ = range(4)

STEPS = [(1, 0, q * QB, QB, T) for q in range(NQ)]
STEPS += [(p, t, 0, GB, T // p) for p in range(2, MAX_SKIP + 1) for t in range(p)]
LAST = len(STEPS) - 1


def gates_of(s):
    return (I_, G_, O_) if STEPS[s][1] == 0 else (I_, G_, F_, O_)


def plan():
    cell = []
    for s in range(len(STEPS)):
        t = STEPS[s][1]
        cell.append([("cell_x", s)] if t == 0 else [("cell_h", s)])
        if s < LAST and STEPS[s + 1][1] > 0:
            cell[-1].append(("cell_x", s + 1))
    graph = [("graph", q, k) for q in range(NQ) for k in range(5)]
    mixes = []
    for q in range(NQ):
        m = [("turn", q), ("query", q), ("key", q), ("value", q)]
        m += [("score", q, b) for b in range(QB)] + [("shift", q)]
        m += [("expo", q, 0)]
        for b in range(1, QB):
            m += [("expo", q, b), ("mix", q, b - 1)]
        m += [("mix", q, QB - 1), ("stat2", q), ("out", q)]
        mixes.append(m)
    n = len(mixes[0])
    lag = 5
    fill = [("stat1", 0), ("stat1", 1), ("norm1", 0), ("norm1", 1)]
    for i in range(n + lag):
        if i < n:
            fill.append(mixes[0][i])
        if i >= lag:
            fill.append(mixes[1][i - lag])
    merged, done = [], 0
    for i, f in enumerate(fill):
        merged.append(f)
        while done < len(graph) and (done + 1) * len(fill) <= (i + 1) * len(graph):
            merged.append(graph[done])
            done += 1
    order, done = [], 0
    for i, pieces in enumerate(cell):
        order += pieces
        upto = (i + 1) * len(merged) // len(cell)
        order += merged[done:upto]
        done = upto
    order.append(("cell_out",))
    return order


PLAN = plan()
STREAM = {"cell_x": "cell", "cell_h": "cell", "cell_out": "cell", "graph": "graph"}


def signals(piece):
    kind = piece[0]
    if kind == "graph":
        _, q, k = piece
        evac = ["hi", "lo"] if k == 4 else [k]
        return [("graph_mm", (q, k))] + [("graph_evac", (q, e)) for e in evac]
    if kind in ("cell_x", "cell_h"):
        s = piece[1]
        if kind == "cell_x" and STEPS[s][1] > 0:
            return []
        late = STEPS[s][1] > 0
        out = [(n, (s, c)) for c in gates_of(s) for n in ("gate_mm", "gate_act")]
        out += [("input_done", s)] + [("forget_done", s)] * late + [("cell_done", s)] * late
        return out + [(n, s) for n in ("tanh_done", "hidden_done", "hidden_hi", "hidden_lo")]
    if kind == "cell_out":
        return [(n, q) for q in range(NQ) for n in ("turned_mm", "y_done")]
    if kind in ("stat1", "stat2"):
        n = kind[-1]
        names = ("stats_done", "pair_done", "half_done", "square_done", "eps_done", "rstd_done")
        return [(name, (n, piece[1])) for name in names]
    if kind == "norm1":
        return [("x1_done", piece[1])]
    if kind == "out":
        return [("out_done", piece[1])]
    q = piece[1]
    if kind in ("turn", "query", "key"):
        return [("mix_mm", (kind, q)), ("hi_done", (kind, q)), ("mix_evac", (kind, q))]
    if kind == "value":
        return [("mix_mm", (kind, q)), ("mix_evac", (kind, q))]
    if kind == "score":
        return [("score_mm", (q, piece[2])), ("max_done", (q, piece[2]))]
    if kind == "shift":
        return [("shift_hi", q), ("shift_lo", q), ("mix_mm", (kind, q)), ("mix_evac", (kind, q))]
    if kind == "expo":
        return [("expo_mm", (q, piece[2])), ("expo_done", (q, piece[2]))]
    if kind == "mix":
        key = (q, piece[2])
        return [("mix_mm", key), ("recip_done", key), ("mix_evac", key), ("z_done", key)]
    raise ValueError(kind)


ORDER = {}
for _piece in PLAN:
    for _sem, _key in signals(_piece):
        ORDER.setdefault(_sem, []).append(_key)


def after(sem, key, g):
    return g * len(ORDER[sem]) + (ORDER[sem].index(key) + 2)


def before(sem, key, g):
    return g * len(ORDER[sem]) + (ORDER[sem].index(key) + 1)


def build(nc, x, adj, wg0, bg0, wg1, bg1, wih, whh, bih, bhh, wqkv, out):
    ctx = ExitStack()
    with ctx:
        def sb(name, shape, dt):
            return ctx.enter_context(nc.sbuf_tensor(name, shape, dt))

        def pb(name, shape, dt):
            return ctx.enter_context(nc.psum_tensor(name, shape, dt))

        def sem(name):
            return ctx.enter_context(nc.semaphore(name))

        ident = sb("ident", [P, P], F32)
        ident16 = sb("ident16", [P, P], F16)
        identb = sb("identb", [P, P], BF16)
        ones_row = sb("ones_row", [1, P], F32)
        pick = sb("pick", [2 * QB * HEADS, QB * HEADS, P], BF16)
        minus_half = sb("minus_half", [P, QB], F32)
        half = sb("half", [P, QB], F32)
        adj_sb = sb("adj_sb", [P, T], F32)
        adj_t = sb("adj_t", [P, T], F32)
        mask = sb("mask", [P, T], BF16)
        mask_t = sb("mask_t", [P, T], BF16)
        wg = sb("wg", [P, 2, D], F32)
        bg_rows = sb("bg_rows", [1, 2 * D], F32)
        bg_all = sb("bg_all", [P, 2, D], F32)
        NW = MAX_SKIP * 4
        w_raw = sb("w_raw", [P, 2 * NW, D], F32)
        w_hi = sb("w_hi", [P, 2 * NW, D], F16)
        w_lo = sb("w_lo", [P, 2 * NW, D], F16)
        b_raw = sb("b_raw", [NW, 2, D], F32)
        b_sum = sb("b_sum", [NW, D], F32)
        bias = sb("bias", [P, NW], F32)
        bias_half = sb("bias_half", [P, NW], F32)
        wqkv_sb = sb("wqkv_sb", [P, 3 * D], F32)
        wqkv_hi = sb("wqkv_hi", [P, 3 * D], F16)
        wqkv_lo = sb("wqkv_lo", [P, 3 * D], F16)
        x_in = sb("x_in", [P, NQ, QB, D], F32)
        x_t = sb("x_t", [P, QB, T], F32)
        u = sb("u", [P, QB, D], F32)
        h1_t = sb("h1_t", [P, QB, T], F32)
        h2_hi = sb("h2_hi", [P, GB, T], F16)
        h2_lo = sb("h2_lo", [P, GB, T], F16)
        state_hi = sb("state_hi", [P, GB, T], F16)
        state_lo = sb("state_lo", [P, GB, T], F16)
        run_hi = sb("run_hi", [P, W], F16)
        run_lo = sb("run_lo", [P, W], F16)
        gate = sb("gate", [P, 2, 4, W], F32)
        inp = sb("inp", [P, 2, W], F32)
        forget = sb("forget", [P, 2, W], F32)
        cell = sb("cell", [P, 2, W], F32)
        tanh_c = sb("tanh_c", [P, 2, W], F32)
        hidden = sb("hidden", [P, 2, W], F32)
        y = sb("y", [P, GB, D], F32)
        x1 = sb("x1", [P, GB, D], F32)
        stats = sb("stats", [P, 2, GB, 6], F32)
        mean_sum, mean_gap, squares, squares_eps, half_gap, gap_square, var_eps = (
            sb(n, [P, QB], F32)
            for n in ("mean_sum", "mean_gap", "squares", "squares_eps", "half_gap", "gap_square", "var_eps"))
        mean = sb("mean", [P, 2, GB], F32)
        rstd = sb("rstd", [P, 2, GB], F32)
        x1t_hi = sb("x1t_hi", [P, NQ, W], F16)
        x1t_lo = sb("x1t_lo", [P, NQ, W], F16)
        part = {(n, h): sb(f"{n}_{h}", [P, NQ, W], F16) for n in ("query", "key") for h in ("hi", "lo")}
        query_stack = sb("query_stack", [P, NQ, HEADS, W], F16)
        key_stack = sb("key_stack", [P, NQ, HEADS, W], F16)
        value = sb("value", [P, NQ, QB, HEADS, VW], F32)
        row_max = sb("row_max", [P, NQ, QB * HEADS], F32)
        shift_parts = sb("shift_parts", [P, NQ, 2 * QB * HEADS], BF16)
        shift_t = sb("shift_t", [2 * QB * HEADS, NQ, P], BF16)
        prob_t = sb("prob_t", [P, NQ, 2, HEADS, T], F32)
        recip = sb("recip", [P, NQ, 2, HEADS], F32)
        mixed = sb("mixed", [P, NQ, 2, D], F32)
        z = sb("z", [P, GB, D], F32)
        result = sb("result", [P, GB, D], F32)

        ps_gate = pb("ps_gate", [P, 4, W], F32)
        ps_score = pb("ps_score", [P, HEADS, T], F32)
        ps_expo = pb("ps_expo", [P, HEADS, T], F32)
        ps_mix = pb("ps_mix", [P, W], F32)
        ps_graph = pb("ps_graph", [P, W], F32)

        S = {name: sem(name) for name in ORDER}
        weights_in = sem("weights_in")
        consts_done = sem("consts_done")
        prep_mm = sem("prep_mm")
        prep_act = sem("prep_act")
        prep_dve = sem("prep_dve")
        x_in_done = [sem(f"x_in_done{q}") for q in range(NQ)]
        x_res_done = [sem(f"x_res_done{q}") for q in range(NQ)]
        stack_done = [sem(f"stack_done{q}") for q in range(NQ)]
        out_stored = [sem(f"out_stored{q}") for q in range(NQ)]

        x_quads = x.rearrange("(g q b) t d -> g q t b d", g=NG, q=NQ)
        out_quads = out.rearrange("(g q b) t d -> g q t b d", g=NG, q=NQ)

        def quad(buf, q):
            return buf[:, q * QB:(q + 1) * QB, :]

        def columns(buf, s):
            p, t, b0, nb, nw = STEPS[s]
            return buf[:, b0:b0 + nb, t:(nw - 1) * p + t + 1:p]

        def size(s):
            return STEPS[s][3] * STEPS[s][4]

        def dense(buf, s):
            return buf[:, 0:size(s)].rearrange("p (b w) -> p b w", b=STEPS[s][3])

        def ends_window(s):
            return STEPS[s][1] == STEPS[s][0] - 1

        def owned(eng, names):
            for n in names:
                eng.sem_inc(S[n], 1)

        def run(eng, stages):
            def round_(g_graph, g_cell, g_mix):
                for piece in PLAN:
                    stream = STREAM.get(piece[0], "mix")
                    g = {"graph": g_graph, "cell": g_cell, "mix": g_mix}[stream]
                    if g is not None and piece[0] in stages:
                        stages[piece[0]](g, *piece[1:])
            head = stages.get("head", lambda g_graph, g_cell: None)
            head(0, None)
            round_(0, None, None)
            head(1, 0)
            round_(1, 0, None)
            with eng.Fori(1, NG - 1) as g:
                head(g + 1, g)
                round_(g + 1, g, g - 1)
            head(None, NG - 1)
            round_(None, NG - 1, NG - 2)
            round_(None, None, NG - 1)

        PREP_DVE = 7 + 2 * NW // 4 + 1
        block = ctx.enter_context(nc.Block())

        @block.sync
        def _(sp):
            sp.dma_start(adj_sb[:], adj).then_inc(weights_in, 16)
            sp.dma_start(wg[:, 0, :], wg0).then_inc(weights_in, 16)
            sp.dma_start(wg[:, 1, :], wg1).then_inc(weights_in, 16)
            sp.dma_start(bg_rows[:, 0:D], bg0.rearrange("(a d) -> a d", a=1)).then_inc(weights_in, 16)
            sp.dma_start(bg_rows[:, D:2 * D], bg1.rearrange("(a d) -> a d", a=1)).then_inc(weights_in, 16)
            sp.dma_start(b_raw[:, 0, :], bih.rearrange("p (c d) -> (p c) d", c=4)).then_inc(weights_in, 16)
            sp.dma_start(b_raw[:, 1, :], bhh.rearrange("p (c d) -> (p c) d", c=4)).then_inc(weights_in, 16)
            sp.dma_start(wqkv_sb[:], wqkv).then_inc(weights_in, 16)
            sp.dma_start(w_raw[:, 0:NW, :], wih.rearrange("p (c r) d -> r (p c) d", c=4)).then_inc(weights_in, 16)
            sp.dma_start(w_raw[:, NW:2 * NW, :], whh.rearrange("p (c r) d -> r (p c) d", c=4)).then_inc(weights_in, 16)

            def head(g_graph, g_cell):
                if g_graph is not None:
                    for q in range(NQ):
                        if not isinstance(g_graph, int) or g_graph > 0:
                            sp.wait_ge(S["graph_mm"], after("graph_mm", (q, 0), g_graph - 1))
                        sp.dma_start(x_in[:, q, :, :], x_quads[g_graph, q]).then_inc(x_in_done[q], 16)
                if isinstance(g_cell, int) and g_cell == 0:
                    for q in range(NQ):
                        sp.dma_start(quad(y, q), x_quads[0, q]).then_inc(x_res_done[q], 16)

            def norm1(g, q):
                sp.wait_ge(S["x1_done"], after("x1_done", q, g))
                if not isinstance(g, int) or g < NG - 1:
                    sp.dma_start(quad(y, q), x_quads[g + 1, q]).then_inc(x_res_done[q], 16)

            def stack(kind):
                dst_all = query_stack if kind == "query" else key_stack
                halves = ("hi", "hi", "lo", "lo") if kind == "query" else ("hi", "lo", "hi", "lo")

                def go(g, q):
                    sp.wait_ge(S["mix_evac"], after("mix_evac", (kind, q), g))
                    for slot, half in enumerate(halves):
                        for h in range(HEADS):
                            sp.dma_start(dst_all[slot * HD:(slot + 1) * HD, q, h, :],
                                         part[kind, half][h * HD:(h + 1) * HD, q, :]).then_inc(stack_done[q], 16)
                return go

            def store(g, q):
                sp.wait_ge(S["out_done"], after("out_done", q, g))
                sp.dma_start(out_quads[g, q], quad(result, q)).then_inc(out_stored[q], 16)

            run(sp, {"head": head, "norm1": norm1, "query": stack("query"), "key": stack("key"), "out": store})
            for q in range(NQ):
                sp.wait_ge(out_stored[q], 16 * NG)

        @block.gpsimd
        def _(pool):
            owned(pool, ["pair_done", "half_done", "square_done", "eps_done", "rstd_done", "z_done"])
            pool.memset(ident[:], 0.0).then_inc(consts_done, 1)
            pool.memset(pick[:], 0.0).then_inc(consts_done, 1)
            pool.memset(ones_row[:], 1.0).then_inc(consts_done, 1)
            pool.memset(minus_half[:], -0.5).then_inc(consts_done, 1)
            pool.memset(half[:], 0.5).then_inc(consts_done, 1)
            pool.memset(value[:, :, :, :, HD:VW], 1.0).then_inc(consts_done, 1)
            pool.wait_ge(consts_done, 6)
            pool.affine_select(out=ident[:], in_=ident[:], compare_op=ALU.not_equal, fill=1.0, base=0,
                               pattern=[[-1, P]], channel_multiplier=1).then_inc(consts_done, 1)
            n = QB * HEADS
            for part_ in range(2):
                pool.affine_select(out=pick[:], in_=pick[:], compare_op=ALU.not_equal, fill=1.0, base=-part_ * n,
                                   pattern=[[-1, n], [0, P]], channel_multiplier=1).then_inc(consts_done, 1)
                pool.wait_ge(consts_done, 8 + part_)
            pool.tensor_copy(ident16[:], ident[:]).then_inc(consts_done, 1)
            pool.tensor_copy(identb[:], ident[:]).then_inc(consts_done, 1)

            def inverse_root(n):
                def go(g, q):
                    i = int(n) - 1
                    cut = slice(q * QB, (q + 1) * QB)
                    even, odd = (stats[:, i, cut, 3 * h:3 * h + 3] for h in range(2))
                    pool.wait_ge(S["stats_done"], after("stats_done", (n, q), g))
                    pool.tensor_tensor(mean_sum[:], even[:, :, 1], odd[:, :, 1], ALU.add)
                    pool.tensor_tensor(mean_gap[:], even[:, :, 1], odd[:, :, 1], ALU.subtract)
                    pool.tensor_tensor(squares[:], even[:, :, 2], odd[:, :, 2], ALU.add).then_inc(S["pair_done"], 1)
                    pool.wait_ge(S["pair_done"], after("pair_done", (n, q), g))
                    pool.tensor_tensor(mean[:, i, cut], mean_sum[:], half[:], ALU.mult)
                    pool.tensor_scalar(squares_eps[:], squares[:], 1.0 / D, EPS, ALU.mult, ALU.add)
                    pool.tensor_tensor(half_gap[:], mean_gap[:], half[:], ALU.mult).then_inc(S["half_done"], 1)
                    pool.wait_ge(S["half_done"], after("half_done", (n, q), g))
                    pool.tensor_tensor(gap_square[:], half_gap[:], half_gap[:], ALU.mult).then_inc(S["square_done"], 1)
                    pool.wait_ge(S["square_done"], after("square_done", (n, q), g))
                    pool.tensor_tensor(var_eps[:], squares_eps[:], gap_square[:], ALU.add).then_inc(S["eps_done"], 1)
                    pool.wait_ge(S["eps_done"], after("eps_done", (n, q), g))
                    pool.tensor_tensor(rstd[:, i, cut], var_eps[:], minus_half[:],
                                       ALU.pow).then_inc(S["rstd_done"], 1)
                return go

            def residual(g, q, b):
                pool.wait_ge(S["mix_evac"], after("mix_evac", (q, b), g))
                pool.tensor_tensor(z[:, q * QB + b, :], mixed[:, q, b % 2, :], x1[:, q * QB + b, :],
                                   ALU.add).then_inc(S["z_done"], 1)

            run(pool, {"stat1": inverse_root("1"), "stat2": inverse_root("2"), "mix": residual})

        @block.tensor
        def _(pe):
            owned(pe, ["graph_mm", "gate_mm", "turned_mm", "mix_mm", "score_mm", "expo_mm"])
            pe.wait_ge(weights_in, 16 * 10)
            pe.wait_ge(consts_done, 11)
            pe.transpose(ps_score[:, 0, :], adj_sb[:], ident[:])
            pe.matmul(ps_score[:, 2:4, :], ones_row[:], bg_rows[:], start=True, stop=True).then_inc(prep_mm, 1)
            pe.wait_ge(prep_dve, 1)
            pe.transpose(ps_expo[:, 0, 0:NW], b_sum[:], ident[0:NW, 0:NW]).then_inc(prep_mm, 1)
            for n in range(2 * NW // 4):
                if n >= 4:
                    pe.wait_ge(prep_dve, 7 + n - 4 + 1)
                for c in range(4):
                    mm = pe.transpose(ps_gate[:, n % 4, c * P:(c + 1) * P], w_raw[:, 4 * n + c, :], ident[:])
                mm.then_inc(prep_mm, 1)
            pe.wait_ge(prep_dve, PREP_DVE)

            def three(out_, s_hi, s_lo, m_hi, m_lo):
                pe.matmul(out_, s_hi, m_hi, start=True, stop=False)
                pe.matmul(out_, s_lo, m_hi, start=False, stop=False)
                return pe.matmul(out_, s_hi, m_lo, start=False, stop=True)

            def graph(g, q, k):
                pe.wait_ge(S["graph_evac"], before("graph_evac", (q, "hi" if k == 4 else k), g))
                if k == 0:
                    pe.wait_ge(x_in_done[q], g * 16 + 16)
                for b in range(QB):
                    o = ps_graph[:, b * T:(b + 1) * T]
                    if k == 0:
                        mm = pe.transpose(o, x_in[:, q, b, :], ident[:])
                    elif k == 1:
                        mm = pe.matmul(o, x_t[:, b, :], wg[:, 0, :], start=True, stop=True)
                    elif k == 3:
                        mm = pe.matmul(o, h1_t[:, b, :], wg[:, 1, :], start=True, stop=True)
                    else:
                        mm = pe.matmul(o, u[:, b, :], adj_t[:], start=True, stop=True)
                mm.then_inc(S["graph_mm"], 1)

            def bank_before(s, c, g):
                for r in range(s - 1, -1, -1):
                    if c in gates_of(r):
                        return after("gate_act", (r, c), g)
                for r in range(LAST, -1, -1):
                    if c in gates_of(r):
                        return after("gate_act", (r, c), g - 1)

            def cell_x(g, s):
                p, t, b0, nb, nw = STEPS[s]
                if s < NQ:
                    pe.wait_ge(S["graph_evac"], after("graph_evac", (s, "lo"), g))
                    pe.wait_ge(S["y_done"], before("y_done", 0, g))
                elif t == 0:
                    pe.wait_ge(S["hidden_lo"], after("hidden_lo", s - 1, g))
                src_hi, src_lo = (h2_hi, h2_lo) if s < NQ else (state_hi, state_lo)
                for c in gates_of(s):
                    if not (isinstance(g, int) and g == 0) or any(c in gates_of(r) for r in range(s)):
                        pe.wait_ge(S["gate_act"], bank_before(s, c, g))
                    o = ps_gate[:, c, 0:size(s)]
                    w = (p - 1) * 4 + c
                    pe.matmul(o, w_hi[:, w, :], columns(src_hi, s), start=True, stop=False)
                    pe.matmul(o, w_lo[:, w, :], columns(src_hi, s), start=False, stop=False)
                    mm = pe.matmul(o, w_hi[:, w, :], columns(src_lo, s), start=False, stop=t == 0)
                    if t == 0:
                        mm.then_inc(S["gate_mm"], 1)

            def cell_h(g, s):
                p = STEPS[s][0]
                n = size(s)
                pe.wait_ge(S["hidden_hi"], after("hidden_hi", s - 1, g))
                for c in gates_of(s):
                    w = NW + (p - 1) * 4 + c
                    pe.matmul(ps_gate[:, c, 0:n], w_hi[:, w, :], run_hi[:, 0:n], start=False, stop=False)
                    pe.matmul(ps_gate[:, c, 0:n], w_lo[:, w, :], run_hi[:, 0:n], start=False, stop=False)
                pe.wait_ge(S["hidden_lo"], after("hidden_lo", s - 1, g))
                for c in gates_of(s):
                    w = NW + (p - 1) * 4 + c
                    pe.matmul(ps_gate[:, c, 0:n], w_hi[:, w, :], run_lo[:, 0:n], start=False,
                              stop=True).then_inc(S["gate_mm"], 1)

            def cell_out(g):
                pe.wait_ge(S["hidden_lo"], after("hidden_lo", LAST, g))
                pe.wait_ge(S["gate_act"], after("gate_act", (LAST, gates_of(LAST)[-1]), g))
                for q in range(NQ):
                    for b in range(QB):
                        o = ps_gate[:, q, b * T:(b + 1) * T]
                        pe.matmul(o, state_hi[:, q * QB + b, :], ident16[:], start=True, stop=False)
                        mm = pe.matmul(o, state_lo[:, q * QB + b, :], ident16[:], start=False, stop=True)
                    mm.then_inc(S["turned_mm"], 1)

            def turn(g, q):
                pe.wait_ge(S["x1_done"], after("x1_done", q, g))
                pe.wait_ge(S["mix_evac"], before("mix_evac", ("turn", q), g))
                for b in range(QB):
                    mm = pe.transpose(ps_mix[:, b * T:(b + 1) * T], x1[:, q * QB + b, :], ident[:])
                mm.then_inc(S["mix_mm"], 1)

            def project(kind):
                def go(g, q):
                    pe.wait_ge(S["mix_evac"], before("mix_evac", (kind, q), g))
                    c = slice(0, D) if kind == "query" else slice(D, 2 * D)
                    three(ps_mix[:], wqkv_hi[:, c], wqkv_lo[:, c], x1t_hi[:, q, :],
                          x1t_lo[:, q, :]).then_inc(S["mix_mm"], 1)
                return go

            def project_value(g, q):
                pe.wait_ge(S["mix_evac"], before("mix_evac", ("value", q), g))
                c = slice(2 * D, 3 * D)
                for b in range(QB):
                    t = slice(b * T, (b + 1) * T)
                    mm = three(ps_mix[:, t], x1t_hi[:, q, t], x1t_lo[:, q, t], wqkv_hi[:, c], wqkv_lo[:, c])
                mm.then_inc(S["mix_mm"], 1)

            def score(g, q, b):
                pe.wait_ge(stack_done[q], (g * 2 + 2) * 16 * HEADS * 4)
                pe.wait_ge(S["max_done"], before("max_done", (q, b), g))
                t = slice(b * T, (b + 1) * T)
                pe.matmul(ps_score[:], identb[:], mask[:, None, :].to_broadcast([P, HEADS, T]),
                          start=True, stop=False, skip_group_check=True)
                for h in range(HEADS):
                    mm = pe.matmul(ps_score[:, h, :], query_stack[:, q, h, t], key_stack[:, q, h, t],
                                   start=False, stop=h == HEADS - 1, skip_group_check=True)
                mm.then_inc(S["score_mm"], 1)

            def shift(g, q):
                pe.wait_ge(S["shift_lo"], after("shift_lo", q, g))
                pe.wait_ge(S["mix_evac"], before("mix_evac", ("shift", q), g))
                pe.transpose(ps_mix[:].bitcast(BF16)[0:2 * QB * HEADS, 0:P], shift_parts[:, q, :],
                             identb[:]).then_inc(S["mix_mm"], 1)

            def expo(g, q, b):
                pe.wait_ge(S["mix_evac"], after("mix_evac", ("shift", q), g))
                pe.wait_ge(S["expo_done"], before("expo_done", (q, b), g))
                t = slice(b * T, (b + 1) * T)
                pe.matmul(ps_expo[:], identb[:], mask_t[:, None, :].to_broadcast([P, HEADS, T]),
                          start=True, stop=False, skip_group_check=True)
                for h in range(HEADS):
                    pe.matmul(ps_expo[:, h, :], key_stack[:, q, h, t], query_stack[:, q, h, t],
                              start=False, stop=False, skip_group_check=True)
                    mm = pe.matmul(ps_expo[:, h, :], pick[:, b * HEADS + h, :], shift_t[:, q, :],
                                   start=False, stop=h == HEADS - 1, skip_group_check=True)
                mm.then_inc(S["expo_mm"], 1)

            def mix(g, q, b):
                pe.wait_ge(S["expo_done"], after("expo_done", (q, b), g))
                pe.wait_ge(S["mix_evac"], before("mix_evac", (q, b), g))
                v = value[:, q, b, :, :].rearrange("p h v -> p (h v)")
                for h in range(HEADS):
                    lead = 0 if h < 2 else VW
                    at = h * VSTEP - (h * VW - lead)
                    mm = pe.matmul(ps_mix[:, at:at + VSPAN], prob_t[:, q, b % 2, h, :], v[:, lead:lead + VSPAN],
                                   start=True, stop=True)
                mm.then_inc(S["mix_mm"], 1)

            run(pe, {"graph": graph, "cell_x": cell_x, "cell_h": cell_h, "cell_out": cell_out, "turn": turn,
                     "query": project("query"), "key": project("key"), "value": project_value, "score": score,
                     "shift": shift, "expo": expo, "mix": mix})

        @block.scalar
        def _(act):
            owned(act, ["gate_act", "tanh_done", "hi_done", "expo_done"])
            for n in range(2 * NW // 4):
                act.wait_ge(prep_mm, 3 + n)
                act.activation(w_hi[:, 4 * n:4 * n + 4, :], ps_gate[:, n % 4, :].rearrange("p (c d) -> p c d", c=4),
                               ACT.Copy, scale=1.0 if n == 0 else 0.5).then_inc(prep_act, 1)
            act.activation(wqkv_hi[:], wqkv_sb[:], ACT.Copy).then_inc(prep_act, 1)

            def graph(g, q, k):
                if k in (0, 2, 4):
                    act.wait_ge(S["graph_mm"], after("graph_mm", (q, k), g))
                src = ps_graph[:].rearrange("p (b t) -> p b t", b=QB)
                if k == 0:
                    act.activation(x_t[:], src, ACT.Copy).then_inc(S["graph_evac"], 1)
                elif k == 2:
                    act.activation(h1_t[:], src, ACT.Relu).then_inc(S["graph_evac"], 1)
                elif k == 4:
                    act.activation(quad(h2_hi, q), src, ACT.Relu).then_inc(S["graph_evac"], 1)

            def elementwise(g, s):
                p, a, n = STEPS[s][0], s % 2, size(s)
                if s < 2 and not (isinstance(g, int) and g == 0):
                    act.wait_ge(S["hidden_lo"], after("hidden_lo", LAST, g - 1))
                for c in gates_of(s):
                    act.wait_ge(S["gate_mm"], after("gate_mm", (s, c), g))
                    w = (p - 1) * 4 + c
                    bc, scale = (bias, 1.0) if c == G_ else (bias_half, 0.5)
                    act.activation(gate[:, a, c, 0:n], ps_gate[:, c, 0:n], ACT.Tanh, bias=bc[:, w:w + 1],
                                   scale=scale).then_inc(S["gate_act"], 1)
                if STEPS[s][1] == 0:
                    act.wait_ge(S["input_done"], after("input_done", s, g))
                else:
                    act.wait_ge(S["cell_done"], after("cell_done", s, g))
                act.activation(tanh_c[:, a, 0:n], cell[:, a, 0:n], ACT.Tanh, scale=0.5).then_inc(S["tanh_done"], 1)

            def cell_x(g, s):
                if STEPS[s][1] == 0:
                    elementwise(g, s)

            def high(kind):
                def go(g, q):
                    dst = x1t_hi if kind == "turn" else part[kind, "hi"]
                    act.wait_ge(S["mix_mm"], after("mix_mm", (kind, q), g))
                    act.activation(dst[:, q, :], ps_mix[:], ACT.Copy).then_inc(S["hi_done"], 1)
                return go

            def expo(g, q, b):
                act.wait_ge(S["expo_mm"], after("expo_mm", (q, b), g))
                act.activation(prob_t[:, q, b % 2, :, :], ps_expo[:], ACT.Exp,
                               scale=HD ** -0.5).then_inc(S["expo_done"], 1)

            act.wait_ge(prep_dve, PREP_DVE)
            run(act, {"graph": graph, "cell_x": cell_x, "cell_h": elementwise, "turn": high("turn"),
                      "query": high("query"), "key": high("key"), "expo": expo})



        @block.vector
        def _(dve):
            owned(dve, ["graph_evac", "input_done", "forget_done", "cell_done", "hidden_done", "hidden_hi", "hidden_lo", "y_done", "stats_done",
                        "x1_done", "out_done", "mix_evac", "max_done", "shift_hi", "shift_lo",
                        "recip_done"])
            dve.wait_ge(weights_in, 16 * 10)
            dve.tensor_tensor(b_sum[:], b_raw[:, 0, :], b_raw[:, 1, :], ALU.add).then_inc(prep_dve, 1)
            dve.tensor_scalar(mask[:], adj_sb[:], 0.0, MASKED, ALU.is_equal, ALU.mult).then_inc(prep_dve, 1)
            dve.wait_ge(prep_mm, 1)
            dve.tensor_scalar(mask_t[:], ps_score[:, 0, :], 0.0, MASKED, ALU.is_equal,
                              ALU.mult).then_inc(prep_dve, 1)
            dve.tensor_copy(adj_t[:], ps_score[:, 0, :]).then_inc(prep_dve, 1)
            dve.tensor_copy(bg_all[:], ps_score[:, 2:4, :]).then_inc(prep_dve, 1)
            dve.wait_ge(prep_mm, 2)
            dve.tensor_copy(bias[:], ps_expo[:, 0, 0:NW]).then_inc(prep_dve, 1)
            dve.tensor_scalar(bias_half[:], ps_expo[:, 0, 0:NW], 0.5, None, ALU.mult).then_inc(prep_dve, 1)
            for n in range(2 * NW // 4):
                dve.wait_ge(prep_act, n + 1)
                dve.scalar_tensor_tensor(out=w_lo[:, 4 * n:4 * n + 4, :],
                                         in0=ps_gate[:, n % 4, :].rearrange("p (c d) -> p c d", c=4),
                                         scalar=1.0 if n == 0 else 0.5, in1=w_hi[:, 4 * n:4 * n + 4, :],
                                         op0=ALU.mult, op1=ALU.subtract).then_inc(prep_dve, 1)
            dve.wait_ge(prep_act, 2 * NW // 4 + 1)
            dve.tensor_tensor(wqkv_lo[:], wqkv_sb[:], wqkv_hi[:], ALU.subtract).then_inc(prep_dve, 1)
            dve.wait_ge(prep_dve, PREP_DVE)

            def graph(g, q, k):
                src = ps_graph[:].rearrange("p (b t) -> p b t", b=QB)
                if k in (1, 3):
                    dve.wait_ge(S["graph_mm"], after("graph_mm", (q, k), g))
                    dve.tensor_tensor(u[:], src, bg_all[:, k // 2, None, :].to_broadcast([P, QB, D]),
                                      ALU.add).then_inc(S["graph_evac"], 1)
                elif k == 4:
                    dve.wait_ge(S["graph_evac"], after("graph_evac", (q, "hi"), g))
                    dve.scalar_tensor_tensor(out=quad(h2_lo, q), in0=src, scalar=0.0, in1=quad(h2_hi, q),
                                             op0=ALU.max, op1=ALU.subtract).then_inc(S["graph_evac"], 1)

            def elementwise(g, s):
                a, n = s % 2, size(s)
                late = STEPS[s][1] > 0
                dve.wait_ge(S["gate_act"], after("gate_act", (s, G_), g))
                dve.scalar_tensor_tensor(out=(inp if late else cell)[:, a, 0:n], in0=gate[:, a, I_, 0:n], scalar=1.0,
                                         in1=gate[:, a, G_, 0:n], op0=ALU.add,
                                         op1=ALU.mult).then_inc(S["input_done"], 1)
                if late:
                    dve.wait_ge(S["gate_act"], after("gate_act", (s, F_), g))
                    dve.scalar_tensor_tensor(out=forget[:, a, 0:n], in0=gate[:, a, F_, 0:n], scalar=1.0,
                                             in1=cell[:, 1 - a, 0:n], op0=ALU.add,
                                             op1=ALU.mult).then_inc(S["forget_done"], 1)
                    dve.wait_ge(S["forget_done"], after("forget_done", s, g))
                    dve.scalar_tensor_tensor(out=cell[:, a, 0:n], in0=forget[:, a, 0:n], scalar=0.5,
                                             in1=inp[:, a, 0:n], op0=ALU.mult,
                                             op1=ALU.add).then_inc(S["cell_done"], 1)
                dve.wait_ge(S["tanh_done"], after("tanh_done", s, g))
                dve.scalar_tensor_tensor(out=hidden[:, a, 0:n], in0=gate[:, a, O_, 0:n], scalar=1.0,
                                         in1=tanh_c[:, a, 0:n], op0=ALU.add,
                                         op1=ALU.mult).then_inc(S["hidden_done"], 1)
                ends = ends_window(s)
                hi = columns(state_hi, s) if ends else dense(run_hi, s)
                lo = columns(state_lo, s) if ends else dense(run_lo, s)
                dve.wait_ge(S["hidden_done"], after("hidden_done", s, g))
                dve.tensor_copy(hi, dense(hidden[:, a, :], s)).then_inc(S["hidden_hi"], 1)
                dve.wait_ge(S["hidden_hi"], after("hidden_hi", s, g))
                dve.tensor_tensor(lo, dense(hidden[:, a, :], s), hi, ALU.subtract).then_inc(S["hidden_lo"], 1)

            def cell_x(g, s):
                if STEPS[s][1] == 0:
                    elementwise(g, s)

            def cell_out(g):
                for q in range(NQ):
                    dve.wait_ge(x_res_done[q], g * 16 + 16)
                    dve.wait_ge(S["turned_mm"], after("turned_mm", q, g))
                    dve.scalar_tensor_tensor(out=quad(y, q), in0=ps_gate[:, q, :].rearrange("p (b d) -> p b d", b=QB),
                                             scalar=0.5, in1=quad(y, q), op0=ALU.mult,
                                             op1=ALU.add).then_inc(S["y_done"], 1)

            def moments_of(n):
                def go(g, q):
                    i = int(n) - 1
                    src = y if n == "1" else z
                    if n == "1":
                        dve.wait_ge(S["y_done"], after("y_done", q, g))
                    else:
                        dve.wait_ge(S["z_done"], after("z_done", (q, QB - 1), g))
                    for b in range(q * QB, (q + 1) * QB):
                        ins = dve.bn_stats(stats[:, i, b, :], src[:, b, :])
                    ins.then_inc(S["stats_done"], 1)
                return go

            def normalise(n):
                def go(g, q):
                    i = int(n) - 1
                    src, dst, done = (y, x1, "x1_done") if n == "1" else (z, result, "out_done")
                    dve.wait_ge(S["rstd_done"], after("rstd_done", (n, q), g))
                    if n == "2" and not (isinstance(g, int) and g == 0):
                        dve.wait_ge(out_stored[q], g * 16)
                    if n == "1" and not (isinstance(g, int) and g == 0):
                        dve.wait_ge(S["z_done"], before("z_done", ORDER["z_done"][0], g))
                    for b in range(q * QB, (q + 1) * QB):
                        ins = dve.tensor_scalar(dst[:, b, :], src[:, b, :], mean[:, i, b:b + 1], rstd[:, i, b:b + 1],
                                                ALU.subtract, ALU.mult)
                    ins.then_inc(S[done], 1)
                return go

            def low(kind):
                def go(g, q):
                    hi, lo = (x1t_hi, x1t_lo) if kind == "turn" else (part[kind, "hi"], part[kind, "lo"])
                    dve.wait_ge(S["hi_done"], after("hi_done", (kind, q), g))
                    dve.tensor_tensor(lo[:, q, :], ps_mix[:], hi[:, q, :], ALU.subtract).then_inc(S["mix_evac"], 1)
                return go

            def take_value(g, q):
                dve.wait_ge(S["mix_mm"], after("mix_mm", ("value", q), g))
                dve.tensor_copy(value[:, q, :, :, 0:HD],
                                ps_mix[:].rearrange("p (b h d) -> p b h d", b=QB, h=HEADS)).then_inc(S["mix_evac"], 1)

            def row_maxima(g, q, b):
                dve.wait_ge(S["score_mm"], after("score_mm", (q, b), g))
                dve.tensor_reduce(row_max[:, q, b * HEADS:(b + 1) * HEADS], ps_score[:], AX_X,
                                  ALU.max).then_inc(S["max_done"], 1)

            def shift(g, q):
                n = QB * HEADS
                dve.wait_ge(S["max_done"], after("max_done", (q, QB - 1), g))
                dve.tensor_scalar(shift_parts[:, q, 0:n], row_max[:, q, :], -1.0, None,
                                  ALU.mult).then_inc(S["shift_hi"], 1)
                dve.wait_ge(S["shift_hi"], after("shift_hi", q, g))
                dve.scalar_tensor_tensor(out=shift_parts[:, q, n:2 * n], in0=row_max[:, q, :], scalar=-1.0,
                                         in1=shift_parts[:, q, 0:n], op0=ALU.mult,
                                         op1=ALU.subtract).then_inc(S["shift_lo"], 1)
                dve.wait_ge(S["mix_mm"], after("mix_mm", ("shift", q), g))
                dve.tensor_copy(shift_t[:, q, :],
                                ps_mix[:].bitcast(BF16)[0:2 * n, 0:P]).then_inc(S["mix_evac"], 1)

            def mix(g, q, b):
                heads = ps_mix[:, 0:(HEADS - 1) * VSTEP + VW]
                dve.wait_ge(S["mix_mm"], after("mix_mm", (q, b), g))
                dve.reciprocal(recip[:, q, b % 2, :], heads[:, HD::VSTEP]).then_inc(S["recip_done"], 1)
                dve.wait_ge(S["recip_done"], after("recip_done", (q, b), g))
                dve.wait_ge(S["z_done"], before("z_done", (q, b), g))
                for h in range(HEADS):
                    ins = dve.tensor_scalar(mixed[:, q, b % 2, h * HD:(h + 1) * HD], ps_mix[:, h * VSTEP:h * VSTEP + HD],
                                            recip[:, q, b % 2, h:h + 1], None, ALU.mult)
                ins.then_inc(S["mix_evac"], 1)

            run(dve, {"graph": graph, "cell_x": cell_x, "cell_h": elementwise, "cell_out": cell_out,
                      "stat1": moments_of("1"), "norm1": normalise("1"), "turn": low("turn"), "query": low("query"),
                      "key": low("key"), "value": take_value, "score": row_maxima, "shift": shift, "mix": mix,
                      "stat2": moments_of("2"), "out": normalise("2")})


INPUTS = ["x", "adj", "L0_gnn_Wg0", "L0_gnn_bg0", "L0_gnn_Wg1", "L0_gnn_bg1", "L0_gnn_Wih", "L0_gnn_Whh",
          "L0_gnn_bih", "L0_gnn_bhh", "L1_gnn_W"]


def kernel(**inputs):
    import concourse.bacc as bacc
    from concourse.bass_utils import run_bass_kernel_spmd

    nc = bacc.Bacc("TRN2", target_bir_lowering=False, num_devices=1)
    arrays, args = {}, []
    for name in INPUTS:
        a = np.ascontiguousarray(inputs[name])
        arrays[f"in_{name}"] = a
        args.append(nc.dram_tensor(f"in_{name}", a.shape, mybir.dt.from_np(a.dtype), kind="ExternalInput").ap())
    args.append(nc.dram_tensor("out_0", (B, T, D), F32, kind="ExternalOutput").ap())
    build(nc, *args)
    r = run_bass_kernel_spmd(nc, [arrays], core_ids=[0])
    return r.results[0]["out_0"]
```

```python
from contextlib import ExitStack

import numpy as np

import concourse.bass as bass
from concourse import mybir

F32 = mybir.dt.float32
F16 = mybir.dt.float16
BF16 = mybir.dt.bfloat16
ALU = mybir.AluOpType
ACT = mybir.ActivationFunctionType
AX_X = mybir.AxisListType.X

P = 128
B, T, D = 128, 128, 128
GB = 16
QB = 4
NQ = GB // QB
NG = B // GB
W = QB * T
HEADS, HD = 4, 32
MAX_SKIP = 4
CHAINS = 2
CB = GB // CHAINS
EPS = 1e-5
MASKED = -1e30
SLOTS = 3
VW = HD + 1
GATE_BANKS = 3
MIX_BANKS = 2
I_, F_, G_, O_ = range(4)

STEPS = [(1, 0, b, QB, T) for b in range(0, CB, QB)]
STEPS += [(p, t, 0, CB, T // p) for p in range(2, MAX_SKIP + 1) for t in range(p)]
LAST = len(STEPS) - 1


def gates_of(s):
    return (I_, G_, O_) if STEPS[s][1] == 0 else (I_, G_, F_, O_)


HEAD, START, FULL, END, TAIL = range(5)
LAG = {"graph": 0, "cell": 1, "mix": 2}

PACE = {
    HEAD: {
        "graph": [(0.0, 1.0), (0.5, 1.0), (5.0, 1.0), (5.5, 1.0)],
    },
    START: {
        "graph": [(0.3, 2.07), (1.3, 2.0), (10.3, 2.0), (11.3, 2.0)],
        "tanh": 0.258,
        "end": 0.398,
    },
    FULL: {
        "first": [(0.0, 0.42), (4.6, 0.51)],
        "attend": [(9.0, 0.5), (11.9, 0.58), (14.3, 0.5), (16.34, 0.47)],
        "graph": [(0.3, 2.0), (1.3, 2.0), (10.3, 2.0), (11.3, 1.44)],
        "tanh": 0.308,
        "end": 0.781,
    },
    END: {
        "first": [(0.0, 0.3), (5.03, 0.51)],
        "attend": [(9.0, 0.68), (11.9, 0.58), (14.3, 0.5), (16.48, 0.45)],
        "tanh": 0.148,
        "end": 0.799,
    },
    TAIL: {
        "first": [(0.0, 0.4), (3.03, 0.39)],
        "attend": [(6.0, 0.55), (8.0, 0.55), (12.0, 0.55), (14.05, 0.55)],
    },
}


def plan(pace):
    timed = []
    n = 0
    if "tanh" in pace:
        for s in range(len(STEPS)):
            for c in range(CHAINS):
                timed += [(n, ("cell_mm", c, s)), (n + pace["tanh"], ("cell_tanh", c, s)),
                          (n + pace["end"], ("cell_end", c, s))]
                n += 1
        timed += [(n - 1 + pace["end"] + 0.01 * (q + 1), (kind, q)) for q in range(NQ)
                  for kind in ("cell_out", "stat1")]
    for i, (start, step) in enumerate(pace.get("first", [])):
        pieces = [(kind, q) for kind in ("norm1", "turn", "query", "key", "value") for q in (2 * i, 2 * i + 1)]
        timed += [(start + k * step, piece) for k, piece in enumerate(pieces)]
    for q, (start, step) in enumerate(pace.get("attend", [])):
        pieces = [("score", q, b) for b in range(QB)] + [("shift", q), ("expo", q, 0)]
        pieces += [("expo", q, 1), ("expo", q, 2), ("mix", q, 0), ("expo", q, 3), ("mix", q, 1), ("stat2", q), ("out", q)]
        timed += [(start + k * step, piece) for k, piece in enumerate(pieces)]
    for q, (start, step) in enumerate(pace.get("graph", [])):
        timed += [(start + k * step, ("graph", q, k)) for k in range(5)]
    order = [piece for _, piece in sorted(timed, key=lambda item: item[0])]
    at = {piece: i for i, piece in enumerate(order)}
    if "attend" in pace:
        for q in range(1, NQ):
            assert all(at["expo", q, b] > at["mix", q - 1, b // 2] for b in range(QB))
        for q in range(2, NQ):
            assert at["mix", q, 0] > at["out", q - 2] and at["turn", q] > at["value", q - 2]
    if "graph" in pace:
        for q in range(2, NQ):
            assert at["graph", q, 0] > at["graph", q - 2, 4]
        if "tanh" in pace:
            per_chain = CB // QB
            assert all(at["graph", q, 4] > at["cell_mm", q // per_chain, q % per_chain] for q in range(NQ))
    return order


PLANS = {kind: plan(PACE[kind]) for kind in PACE}
STREAM = {"cell_mm": "cell", "cell_out": "cell", "cell_tanh": "cell", "cell_end": "cell", "stat1": "cell", "graph": "graph"}


def signals(piece):
    kind = piece[0]
    if kind == "graph":
        _, q, k = piece
        evac = ["hi", "lo"] if k == 4 else [k]
        return [("graph_mm", (q, k))] + [(f"graph_evac{q % 2}", (q, e)) for e in evac]
    if kind == "cell_mm":
        key = piece[1:]
        late = STEPS[key[1]][1] > 0
        out = [(n, (*key, c)) for c in gates_of(key[1]) for n in ("gate_mm", "gate_act")]
        return out + [("input_done", key)] + [("forget_done", key)] * late + [("cell_done", key)] * late
    if kind == "cell_tanh":
        return [("tanh_done", piece[1:])]
    if kind == "cell_end":
        return [(n, piece[1:]) for n in ("hidden_done", "hidden_hi", "hidden_lo")]
    if kind == "cell_out":
        return [(n, piece[1]) for n in ("turned_mm", "y_done")]
    if kind in ("stat1", "stat2"):
        n = kind[-1]
        names = ("stats_done", "pair_done", "half_done", "square_done", "eps_done", "rstd_done")
        return [(name + n, piece[1]) for name in names]
    if kind == "norm1":
        return [("x1_done", piece[1])]
    if kind == "out":
        return [("out_done", piece[1])]
    q = piece[1]
    if kind in ("turn", "query", "key", "value"):
        return [("mix_mm", (kind, q)), ("hi_done", (kind, q)), ("mix_evac", (kind, q))]
    if kind == "score":
        return [("score_mm", (q, piece[2])), ("max_done", (q, piece[2]))]
    if kind == "shift":
        return [("shift_hi", q), ("shift_lo", q), ("mix_mm", (kind, q)), ("mix_evac", (kind, q))]
    if kind == "expo":
        return [("expo_mm", (q, piece[2])), ("expo_done", (q, piece[2])), ("prob_lo_done", (q, piece[2]))]
    if kind == "mix":
        key = (q, piece[2])
        return [("mix_mm", key), ("recip_done", key), ("mix_evac", key), ("z_done", key)]
    raise ValueError(kind)


def stream_of(piece):
    return STREAM.get(piece[0], "mix")


ORDER, STREAM_OF = {}, {}
for _kind, _plan in PLANS.items():
    for _piece in _plan:
        for _sem, _key in signals(_piece):
            ORDER.setdefault((_sem, _kind), []).append(_key)
            STREAM_OF[_sem] = stream_of(_piece)
COUNT = {sem: len(ORDER[sem, FULL]) for sem in STREAM_OF}
assert COUNT["gate_mm"] % GATE_BANKS == 0 and COUNT["mix_mm"] % MIX_BANKS == 0


def order_of(sem, g):
    if not isinstance(g, int):
        return ORDER[sem, FULL]
    r = g + LAG[STREAM_OF[sem]]
    return ORDER[sem, HEAD if r == 0 else START if r == 1 else FULL if r < NG else END if r == NG else TAIL]


def after(sem, key, g):
    return g * COUNT[sem] + (order_of(sem, g).index(key) + 2)


def before(sem, key, g):
    return g * COUNT[sem] + (order_of(sem, g).index(key) + 1)


def bank_free(sem, banks, key, g):
    return g * COUNT[sem] + (order_of(sem, g).index(key) + 2 - banks)


def build(nc, x, adj, wg0, bg0, wg1, bg1, wih, whh, bih, bhh, wqkv, out):
    ctx = ExitStack()
    with ctx:
        def sb(name, shape, dt):
            return ctx.enter_context(nc.sbuf_tensor(name, shape, dt))

        def pb(name, shape, dt):
            return ctx.enter_context(nc.psum_tensor(name, shape, dt))

        def sem(name):
            return ctx.enter_context(nc.semaphore(name))

        ident = sb("ident", [P, P], F32)
        ident16 = sb("ident16", [P, P], F16)
        identb = sb("identb", [P, P], BF16)
        ones_row = sb("ones_row", [1, P], F32)
        pick = sb("pick", [2 * QB * HEADS, QB * HEADS, P], BF16)
        minus_half = sb("minus_half", [P, QB], F32)
        half = sb("half", [P, QB], F32)
        adj_sb = sb("adj_sb", [P, T], F32)
        adj_t = sb("adj_t", [P, T], F32)
        mask = sb("mask", [P, T], BF16)
        mask_t = sb("mask_t", [P, T], BF16)
        wg = sb("wg", [P, 2, D], F32)
        bg_rows = sb("bg_rows", [1, 2 * D], F32)
        bg_all = sb("bg_all", [P, 2, D], F32)
        NW = MAX_SKIP * 4
        w_hi = sb("w_hi", [P, 2 * NW, D], F16)
        w_lo = sb("w_lo", [P, 2 * NW, D], F16)
        b_raw = sb("b_raw", [NW, 2, D], F32)
        b_sum = sb("b_sum", [NW, D], F32)
        bias = sb("bias", [P, NW], F32)
        bias_half = sb("bias_half", [P, NW], F32)
        wqkv_sb = sb("wqkv_sb", [P, 3 * D], F32)
        wqkv_hi = sb("wqkv_hi", [P, 3 * D], F16)
        wqkv_lo = sb("wqkv_lo", [P, 3 * D], F16)
        x_in = sb("x_in", [P, NQ, QB, D], F32)
        x_t = sb("x_t", [P, 2, QB, T], F32)
        u = sb("u", [P, 2, QB, D], F32)
        h1_t = sb("h1_t", [P, 2, QB, T], F32)
        h2_hi = sb("h2_hi", [P, GB, T], F16)
        h2_lo = sb("h2_lo", [P, GB, T], F16)
        state_hi = sb("state_hi", [P, GB, T], F16)
        state_lo = sb("state_lo", [P, GB, T], F16)
        run_hi = sb("run_hi", [P, CHAINS, W], F16)
        run_lo = sb("run_lo", [P, CHAINS, W], F16)
        gate = sb("gate", [P, CHAINS, 4, W], F32)
        inp = sb("inp", [P, CHAINS, W], F32)
        forget = sb("forget", [P, CHAINS, W], F32)
        cell = sb("cell", [P, CHAINS, W], F32)
        tanh_c = sb("tanh_c", [P, CHAINS, W], F32)
        hidden = sb("hidden", [P, CHAINS, W], F32)
        y = sb("y", [P, GB, D], F32)
        x1 = sb("x1", [P, GB, D], F32)
        stats = sb("stats", [P, 2, GB, 6], F32)
        mean_sum, mean_gap, squares, squares_eps, half_gap, gap_square, var_eps = (
            sb(n, [P, QB], F32)
            for n in ("mean_sum", "mean_gap", "squares", "squares_eps", "half_gap", "gap_square", "var_eps"))
        mean = sb("mean", [P, 2, GB], F32)
        rstd = sb("rstd", [P, 2, GB], F32)
        x1t_hi = sb("x1t_hi", [P, 2, W], F16)
        x1t_lo = sb("x1t_lo", [P, 2, W], F16)
        part = {(n, h): sb(f"{n}_{h}", [P, NQ, W], F16) for n in ("query", "key") for h in ("hi", "lo")}
        query_stack = sb("query_stack", [P, 2, HEADS, 2, W], F16)
        w_raw = query_stack[:].rearrange("p a h b w -> p (a h b w)").bitcast(F32).rearrange("p (n d) -> p n d", d=D)
        key_stack = sb("key_stack", [P, 2, HEADS, 2, W], F16)
        value_hi = sb("value_hi", [P, NQ, QB, HEADS, VW], F16)
        value_lo = sb("value_lo", [P, NQ, QB, HEADS, VW], F16)
        row_max = sb("row_max", [P, NQ, QB * HEADS], F32)
        shift_parts = sb("shift_parts", [P, NQ, 2 * QB * HEADS], BF16)
        shift_t = sb("shift_t", [2 * QB * HEADS, NQ, P], BF16)
        prob_t = sb("prob_t", [P, QB, HEADS, T], F32)
        prob_hi = prob_t[:].bitcast(BF16).rearrange("p b h (t two) -> p b h t two", two=2)[:, :, :, :, 1]
        prob_lo = sb("prob_lo", [P, QB, HEADS, T], F16)
        recip = sb("recip", [P, 2, 2 * HEADS], F32)
        mixed = sb("mixed", [P, 2, 2 * HEADS, HD], F32)
        z = sb("z", [P, 2 * QB, D], F32)
        result = sb("result", [P, 2 * QB, D], F32)

        ps_gate = pb("ps_gate", [P, GATE_BANKS, W], F32)
        ps_score = pb("ps_score", [P, HEADS, T], F32)
        ps_expo = pb("ps_expo", [P, HEADS, T], F32)
        ps_mix = pb("ps_mix", [P, MIX_BANKS, W], F32)
        ps_graph = pb("ps_graph", [P, W], F32)

        S = {name: sem(name) for name in STREAM_OF}
        weights_in = sem("weights_in")
        consts_done = sem("consts_done")
        prep_mm = sem("prep_mm")
        prep_act = sem("prep_act")
        prep_dve = sem("prep_dve")
        x_in_done = [sem(f"x_in_done{q}") for q in range(NQ)]
        x_res_done = [sem(f"x_res_done{q}") for q in range(NQ)]
        stack_done = [sem(f"stack_done{pair}") for pair in range(NQ // 2)]
        out_stored = [sem(f"out_stored{r}") for r in range(2)]

        x_quads = x.rearrange("(g q b) t d -> g q t b d", g=NG, q=NQ)
        out_quads = out.rearrange("(g q b) t d -> g q t b d", g=NG, q=NQ)

        def quad(buf, q):
            return buf[:, q * QB:(q + 1) * QB, :]

        def columns(buf, c, s):
            p, t, b0, nb, nw = STEPS[s]
            return buf[:, c * CB + b0:c * CB + b0 + nb, t:(nw - 1) * p + t + 1:p]

        def gate_bank(c, s, i):
            return ps_gate[:, order_of("gate_mm", 0).index((c, s, i)) % GATE_BANKS, 0:size(s)]

        def in_tail(g):
            return isinstance(g, int) and g == NG - 1

        def mix_bank(key, g):
            i = order_of("mix_mm", g).index(key)
            if in_tail(g):
                return [ps_mix[:, 0, :], ps_mix[:, 1, :], ps_graph[:]][i % 3]
            return ps_mix[:, i % MIX_BANKS, :]

        def score_bank(key, g):
            i = order_of("score_mm", g).index(key)
            return flat(ps_score) if not in_tail(g) or i % 2 == 0 else ps_gate[:, 0, :]

        def expo_bank(key, g):
            i = order_of("expo_mm", g).index(key)
            return flat(ps_expo) if not in_tail(g) or i % 2 == 0 else ps_gate[:, 1, :]

        def graph_bank(q, g):
            return flat(ps_score) if isinstance(g, int) and g == 0 and q % 2 else ps_graph[:]

        def flat(bank):
            return bank[:].rearrange("p h t -> p (h t)")

        def size(s):
            return STEPS[s][3] * STEPS[s][4]

        def dense(buf, s):
            return buf[:, 0:size(s)].rearrange("p (b w) -> p b w", b=STEPS[s][3])

        def ends_window(s):
            return STEPS[s][1] == STEPS[s][0] - 1

        def owned(eng, names):
            for n in names:
                eng.sem_inc(S[n], 1)

        def run(eng, stages):
            def round_(kind, **groups):
                for piece in PLANS[kind]:
                    if piece[0] in stages:
                        stages[piece[0]](groups[stream_of(piece)], *piece[1:])
            head = stages.get("head", lambda g_graph, g_cell: None)
            head(0, None)
            round_(HEAD, graph=0)
            head(1, 0)
            round_(START, graph=1, cell=0)
            with eng.Fori(1, NG - 1) as g:
                head(g + 1, g)
                round_(FULL, graph=g + 1, cell=g, mix=g - 1)
            head(None, NG - 1)
            round_(END, cell=NG - 1, mix=NG - 2)
            round_(TAIL, mix=NG - 1)

        PREP_DVE = 7 + 2 * NW // 4 + 1
        block = ctx.enter_context(nc.Block())

        @block.sync
        def _(sp):
            for r in range(2):
                sp.sem_inc(out_stored[r], 16)
            sp.dma_start(adj_sb[:], adj).then_inc(weights_in, 16)
            sp.dma_start(wg[:, 0, :], wg0).then_inc(weights_in, 16)
            sp.dma_start(wg[:, 1, :], wg1).then_inc(weights_in, 16)
            sp.dma_start(bg_rows[:, 0:D], bg0.rearrange("(a d) -> a d", a=1)).then_inc(weights_in, 16)
            sp.dma_start(bg_rows[:, D:2 * D], bg1.rearrange("(a d) -> a d", a=1)).then_inc(weights_in, 16)
            sp.dma_start(b_raw[:, 0, :], bih.rearrange("p (c d) -> (p c) d", c=4)).then_inc(weights_in, 16)
            sp.dma_start(b_raw[:, 1, :], bhh.rearrange("p (c d) -> (p c) d", c=4)).then_inc(weights_in, 16)
            sp.dma_start(wqkv_sb[:], wqkv).then_inc(weights_in, 16)
            sp.dma_start(w_raw[:, 0:NW, :], wih.rearrange("p (c r) d -> r (p c) d", c=4)).then_inc(weights_in, 16)
            sp.dma_start(w_raw[:, NW:2 * NW, :], whh.rearrange("p (c r) d -> r (p c) d", c=4)).then_inc(weights_in, 16)

            def head(g_graph, g_cell):
                if isinstance(g_cell, int) and g_cell == 0:
                    for q in range(NQ):
                        sp.dma_start(quad(y, q), x_quads[0, q]).then_inc(x_res_done[q], 16)

            def norm1(g, q):
                sp.wait_ge(S["x1_done"], after("x1_done", q, g))
                if not isinstance(g, int) or g < NG - 1:
                    sp.dma_start(quad(y, q), x_quads[g + 1, q]).then_inc(x_res_done[q], 16)

            def stack(kind):
                dst_all = query_stack if kind == "query" else key_stack
                halves = ("hi", "hi", "lo") if kind == "query" else ("hi", "lo", "hi")

                def go(g, q):
                    if q % 2 == 0:
                        return
                    sp.wait_ge(S["mix_evac"], after("mix_evac", (kind, q), g))
                    for slot, half in enumerate(halves):
                        for h in range(HEADS):
                            sp.dma_start(dst_all[slot * HD:(slot + 1) * HD, q // 2, h, :, :],
                                         part[kind, half][h * HD:(h + 1) * HD, q - 1:q + 1, :]).then_inc(stack_done[q // 2], 16)
                return go

            def store(g, q):
                sp.wait_ge(S["out_done"], after("out_done", q, g))
                sp.dma_start(out_quads[g, q], quad(result, q % 2)).then_inc(out_stored[q % 2], 16)

            run(sp, {"head": head, "norm1": norm1, "query": stack("query"), "key": stack("key"), "out": store})
            for r in range(2):
                sp.wait_ge(out_stored[r], 16 * (NG * NQ // 2 + 1))

        @block.gpsimd
        def _(pool):
            owned(pool, ["prob_lo_done", "z_done"])
            owned(pool, [name + n for n in "12" for name in ("pair_done", "half_done", "square_done", "eps_done",
                                                             "rstd_done")])
            pool.memset(ident[:], 0.0).then_inc(consts_done, 1)
            pool.memset(pick[:], 0.0).then_inc(consts_done, 1)
            pool.memset(ones_row[:], 1.0).then_inc(consts_done, 1)
            pool.memset(minus_half[:], -0.5).then_inc(consts_done, 1)
            pool.memset(half[:], 0.5).then_inc(consts_done, 1)
            pool.memset(value_hi[:, :, :, :, HD:VW], 1.0).then_inc(consts_done, 1)
            pool.memset(value_lo[:, :, :, :, HD:VW], 0.0).then_inc(consts_done, 1)
            pool.wait_ge(consts_done, 7)
            pool.affine_select(out=ident[:], in_=ident[:], compare_op=ALU.not_equal, fill=1.0, base=0,
                               pattern=[[-1, P]], channel_multiplier=1).then_inc(consts_done, 1)
            n = QB * HEADS
            for part_ in range(2):
                pool.affine_select(out=pick[:], in_=pick[:], compare_op=ALU.not_equal, fill=1.0, base=-part_ * n,
                                   pattern=[[-1, n], [0, P]], channel_multiplier=1).then_inc(consts_done, 1)
                pool.wait_ge(consts_done, 9 + part_)
            pool.tensor_copy(ident16[:], ident[:]).then_inc(consts_done, 1)
            pool.tensor_copy(identb[:], ident[:]).then_inc(consts_done, 1)

            def inverse_root(n):
                def go(g, q):
                    i = int(n) - 1
                    cut = slice(q * QB, (q + 1) * QB)
                    even, odd = (stats[:, i, cut, 3 * h:3 * h + 3] for h in range(2))
                    pool.wait_ge(S["stats_done" + n], after("stats_done" + n, q, g))
                    pool.tensor_tensor(mean_sum[:], even[:, :, 1], odd[:, :, 1], ALU.add)
                    pool.tensor_tensor(mean_gap[:], even[:, :, 1], odd[:, :, 1], ALU.subtract)
                    pool.tensor_tensor(squares[:], even[:, :, 2], odd[:, :, 2], ALU.add).then_inc(S["pair_done" + n], 1)
                    pool.wait_ge(S["pair_done" + n], after("pair_done" + n, q, g))
                    pool.tensor_tensor(mean[:, i, cut], mean_sum[:], half[:], ALU.mult)
                    pool.tensor_scalar(squares_eps[:], squares[:], 1.0 / D, EPS, ALU.mult, ALU.add)
                    pool.tensor_tensor(half_gap[:], mean_gap[:], half[:], ALU.mult).then_inc(S["half_done" + n], 1)
                    pool.wait_ge(S["half_done" + n], after("half_done" + n, q, g))
                    pool.tensor_tensor(gap_square[:], half_gap[:], half_gap[:], ALU.mult).then_inc(S["square_done" + n], 1)
                    pool.wait_ge(S["square_done" + n], after("square_done" + n, q, g))
                    pool.tensor_tensor(var_eps[:], squares_eps[:], gap_square[:], ALU.add).then_inc(S["eps_done" + n], 1)
                    pool.wait_ge(S["eps_done" + n], after("eps_done" + n, q, g))
                    pool.tensor_tensor(rstd[:, i, cut], var_eps[:], minus_half[:],
                                       ALU.pow).then_inc(S["rstd_done" + n], 1)
                return go

            def prob_low(g, q, b):
                pool.wait_ge(S["expo_done"], after("expo_done", (q, b), g))
                pool.tensor_tensor(prob_lo[:, b, :, :], prob_t[:, b, :, :], prob_hi[:, b, :, :],
                                   ALU.subtract).then_inc(S["prob_lo_done"], 1)

            def residual(g, q, m):
                pool.wait_ge(S["mix_evac"], after("mix_evac", (q, m), g))
                pool.tensor_tensor(z[:, (q % 2) * QB + 2 * m:(q % 2) * QB + 2 * m + 2, :],
                                   mixed[:, m, :, :].rearrange("p (b h) d -> p b (h d)", b=2),
                                   x1[:, q * QB + 2 * m:q * QB + 2 * m + 2, :], ALU.add).then_inc(S["z_done"], 1)

            run(pool, {"stat1": inverse_root("1"), "stat2": inverse_root("2"), "expo": prob_low,
                       "mix": residual})

        @block.tensor
        def _(pe):
            owned(pe, ["graph_mm", "gate_mm", "turned_mm", "mix_mm", "score_mm", "expo_mm"])
            pe.wait_ge(weights_in, 16 * 10)
            pe.wait_ge(consts_done, 12)
            pe.transpose(ps_score[:, 0, :], adj_sb[:], ident[:])
            pe.matmul(ps_score[:, 2:4, :], ones_row[:], bg_rows[:], start=True, stop=True).then_inc(prep_mm, 1)
            pe.wait_ge(prep_dve, 1)
            pe.transpose(ps_expo[:, 0, 0:NW], b_sum[:], ident[0:NW, 0:NW]).then_inc(prep_mm, 1)
            for n in range(2 * NW // 4):
                if n >= GATE_BANKS:
                    pe.wait_ge(prep_dve, 7 + n - GATE_BANKS + 1)
                for c in range(4):
                    mm = pe.transpose(ps_gate[:, n % GATE_BANKS, c * P:(c + 1) * P], w_raw[:, 4 * n + c, :], ident[:])
                mm.then_inc(prep_mm, 1)
            pe.wait_ge(prep_dve, PREP_DVE)

            def three(out_, s_hi, s_lo, m_hi, m_lo):
                pe.matmul(out_, s_hi, m_hi, start=True, stop=False)
                pe.matmul(out_, s_lo, m_hi, start=False, stop=False)
                return pe.matmul(out_, s_hi, m_lo, start=False, stop=True)

            def graph(g, q, k):
                own = f"graph_evac{q % 2}"
                if k > 0:
                    pe.wait_ge(S[own], after(own, (q, k - 1), g))
                elif not (isinstance(g, int) and g == 0) or q >= 2:
                    pe.wait_ge(S[own], before(own, (q, 0), g))
                order = order_of("graph_mm", g)
                i = order.index((q, k))
                if not (isinstance(g, int) and g == 0) and order[i - 1][0] % 2 != q % 2:
                    q_, k_ = order[i - 1]
                    other = f"graph_evac{q_ % 2}"
                    pe.wait_ge(S[other], after(other, (q_, "lo" if k_ == 4 else k_), g if i > 0 else g - 1))
                if k == 0:
                    pe.wait_ge(x_in_done[q], g * 16 + 16)
                for b in range(QB):
                    o = graph_bank(q, g)[:, b * T:(b + 1) * T]
                    if k == 0:
                        mm = pe.transpose(o, x_in[:, q, b, :], ident[:])
                    elif k == 1:
                        mm = pe.matmul(o, x_t[:, q % 2, b, :], wg[:, 0, :], start=True, stop=True)
                    elif k == 3:
                        mm = pe.matmul(o, h1_t[:, q % 2, b, :], wg[:, 1, :], start=True, stop=True)
                    else:
                        mm = pe.matmul(o, u[:, q % 2, b, :], adj_t[:], start=True, stop=True)
                mm.then_inc(S["graph_mm"], 1)

            def cell_mm(g, c, s):
                p, t, b0, nb, nw = STEPS[s]
                n = size(s)
                if p == 1:
                    q = (c * CB + b0) // QB
                    pe.wait_ge(S[f"graph_evac{q % 2}"], after(f"graph_evac{q % 2}", (q, "lo"), g))
                    if c == 0 and s == 0:
                        pe.wait_ge(S["y_done"], before("y_done", 0, g))
                else:
                    pe.wait_ge(S["hidden_lo"], after("hidden_lo", (c, s - 1), g))
                src_hi, src_lo = (h2_hi, h2_lo) if p == 1 else (state_hi, state_lo)
                for i in gates_of(s):
                    w = (p - 1) * 4 + i
                    o = gate_bank(c, s, i)
                    if not (isinstance(g, int) and g == 0) or order_of("gate_act", g).index((c, s, i)) >= GATE_BANKS:
                        pe.wait_ge(S["gate_act"], bank_free("gate_act", GATE_BANKS, (c, s, i), g))
                    pe.matmul(o, w_hi[:, w, :], columns(src_hi, c, s), start=True, stop=False)
                    pe.matmul(o, w_lo[:, w, :], columns(src_hi, c, s), start=False, stop=False)
                    mm = pe.matmul(o, w_hi[:, w, :], columns(src_lo, c, s), start=False, stop=t == 0)
                    if t > 0:
                        w += NW
                        pe.matmul(o, w_hi[:, w, :], run_hi[:, c, 0:n], start=False, stop=False)
                        pe.matmul(o, w_lo[:, w, :], run_hi[:, c, 0:n], start=False, stop=False)
                        mm = pe.matmul(o, w_hi[:, w, :], run_lo[:, c, 0:n], start=False, stop=True)
                    mm.then_inc(S["gate_mm"], 1)

            def cell_out(g, q):
                if q == 0:
                    pe.wait_ge(S["hidden_lo"], after("hidden_lo", (CHAINS - 1, LAST), g))
                    pe.wait_ge(S["gate_act"], after("gate_act", (CHAINS - 1, LAST, gates_of(LAST)[-1]), g))
                if q >= GATE_BANKS:
                    pe.wait_ge(S["y_done"], after("y_done", q - GATE_BANKS, g))
                for b in range(QB):
                    o = ps_gate[:, q % GATE_BANKS, b * T:(b + 1) * T]
                    pe.matmul(o, state_hi[:, q * QB + b, :], ident16[:], start=True, stop=False)
                    mm = pe.matmul(o, state_lo[:, q * QB + b, :], ident16[:], start=False, stop=True)
                mm.then_inc(S["turned_mm"], 1)

            def mix_bank_free(key, g):
                banks = 3 if in_tail(g) else MIX_BANKS
                if not (isinstance(g, int) and g == 0) or order_of("mix_evac", g).index(key) >= banks:
                    pe.wait_ge(S["mix_evac"], bank_free("mix_evac", banks, key, g))

            def turn(g, q):
                pe.wait_ge(S["x1_done"], after("x1_done", q, g))
                mix_bank_free(("turn", q), g)
                for b in range(QB):
                    mm = pe.transpose(mix_bank(("turn", q), g)[:, b * T:(b + 1) * T], x1[:, q * QB + b, :], ident[:])
                mm.then_inc(S["mix_mm"], 1)

            def project(kind):
                def go(g, q):
                    pe.wait_ge(S["mix_evac"], after("mix_evac", ("turn", q), g))
                    mix_bank_free((kind, q), g)
                    c = slice(0, D) if kind == "query" else slice(D, 2 * D)
                    three(mix_bank((kind, q), g), wqkv_hi[:, c], wqkv_lo[:, c], x1t_hi[:, q % 2, :],
                          x1t_lo[:, q % 2, :]).then_inc(S["mix_mm"], 1)
                return go

            def project_value(g, q):
                pe.wait_ge(S["mix_evac"], after("mix_evac", ("turn", q), g))
                mix_bank_free(("value", q), g)
                c = slice(2 * D, 3 * D)
                for b in range(QB):
                    t = slice(b * T, (b + 1) * T)
                    mm = three(mix_bank(("value", q), g)[:, t], x1t_hi[:, q % 2, t], x1t_lo[:, q % 2, t], wqkv_hi[:, c], wqkv_lo[:, c])
                mm.then_inc(S["mix_mm"], 1)

            def score(g, q, b):
                pe.wait_ge(stack_done[q // 2], (g * 2 + 2) * 16 * HEADS * SLOTS)
                pe.wait_ge(S["max_done"], bank_free("max_done", 2, (q, b), g) if in_tail(g) else
                           before("max_done", (q, b), g))
                bank = score_bank((q, b), g).rearrange("p (h t) -> p h t", h=HEADS)
                t = slice(b * T, (b + 1) * T)
                pe.matmul(bank, identb[:], mask[:, None, :].to_broadcast([P, HEADS, T]),
                          start=True, stop=False, skip_group_check=True)
                for h in range(HEADS):
                    mm = pe.matmul(bank[:, h, :], query_stack[0:SLOTS * HD, q // 2, h, q % 2, t], key_stack[0:SLOTS * HD, q // 2, h, q % 2, t],
                                   start=False, stop=h == HEADS - 1, skip_group_check=True)
                mm.then_inc(S["score_mm"], 1)

            def shift(g, q):
                pe.wait_ge(S["shift_lo"], after("shift_lo", q, g))
                mix_bank_free(("shift", q), g)
                pe.transpose(mix_bank(("shift", q), g).bitcast(BF16)[0:2 * QB * HEADS, 0:P], shift_parts[:, q, :],
                             identb[:]).then_inc(S["mix_mm"], 1)

            def expo(g, q, b):
                pe.wait_ge(S["mix_evac"], after("mix_evac", ("shift", q), g))
                pe.wait_ge(S["expo_done"], bank_free("expo_done", 2, (q, b), g) if in_tail(g) else
                           before("expo_done", (q, b), g))
                bank = expo_bank((q, b), g).rearrange("p (h t) -> p h t", h=HEADS)
                t = slice(b * T, (b + 1) * T)
                pe.matmul(bank, identb[:], mask_t[:, None, :].to_broadcast([P, HEADS, T]),
                          start=True, stop=False, skip_group_check=True)
                for h in range(HEADS):
                    pe.matmul(bank[:, h, :], key_stack[0:SLOTS * HD, q // 2, h, q % 2, t], query_stack[0:SLOTS * HD, q // 2, h, q % 2, t],
                              start=False, stop=False, skip_group_check=True)
                    mm = pe.matmul(bank[:, h, :], pick[:, b * HEADS + h, :], shift_t[:, q, :],
                                   start=False, stop=h == HEADS - 1, skip_group_check=True)
                mm.then_inc(S["expo_mm"], 1)

            def mix(g, q, m):
                pe.wait_ge(S["prob_lo_done"], after("prob_lo_done", (q, 2 * m + 1), g))
                mix_bank_free((q, m), g)
                for b in range(2 * m, 2 * m + 2):
                    for h in range(HEADS):
                        at = ((b - 2 * m) * HEADS + h) * VW
                        o = mix_bank((q, m), g)[:, at:at + VW]
                        pe.matmul(o, prob_hi[:, b, h, :], value_hi[:, q, b, h, :], start=True, stop=False)
                        pe.matmul(o, prob_hi[:, b, h, :], value_lo[:, q, b, h, :], start=False, stop=False)
                        mm = pe.matmul(o, prob_lo[:, b, h, :], value_hi[:, q, b, h, :], start=False, stop=True)
                mm.then_inc(S["mix_mm"], 1)

            run(pe, {"graph": graph, "cell_mm": cell_mm, "cell_out": cell_out, "turn": turn,
                     "query": project("query"), "key": project("key"), "value": project_value, "score": score,
                     "shift": shift, "expo": expo, "mix": mix})

        @block.scalar
        def _(act):
            owned(act, ["gate_act", "tanh_done", "hi_done", "expo_done"])
            for n in range(2 * NW // 4):
                act.wait_ge(prep_mm, 3 + n)
                act.activation(w_hi[:, 4 * n:4 * n + 4, :], ps_gate[:, n % GATE_BANKS, :].rearrange("p (c d) -> p c d", c=4),
                               ACT.Copy, scale=1.0 if n == 0 else 0.5).then_inc(prep_act, 1)
            act.activation(wqkv_hi[:], wqkv_sb[:], ACT.Copy).then_inc(prep_act, 1)

            def graph(g, q, k):
                if k in (0, 2, 4):
                    act.wait_ge(S["graph_mm"], after("graph_mm", (q, k), g))
                src = graph_bank(q, g).rearrange("p (b t) -> p b t", b=QB)
                if k == 0:
                    act.activation(x_t[:, q % 2, :, :], src, ACT.Copy).then_inc(S[f"graph_evac{q % 2}"], 1)
                elif k == 2:
                    act.activation(h1_t[:, q % 2, :, :], src, ACT.Relu).then_inc(S[f"graph_evac{q % 2}"], 1)
                elif k == 4:
                    act.activation(quad(h2_hi, q), src, ACT.Relu).then_inc(S[f"graph_evac{q % 2}"], 1)

            def gates(g, c, s):
                p, n = STEPS[s][0], size(s)
                for i in gates_of(s):
                    if s == 0 and not (isinstance(g, int) and g == 0) and i == I_:
                        act.wait_ge(S["hidden_lo"], after("hidden_lo", (c, LAST), g - 1))
                    elif 0 < s < CB // QB and i == I_:
                        act.wait_ge(S["hidden_lo"], after("hidden_lo", (c, s - 1), g))
                    act.wait_ge(S["gate_mm"], after("gate_mm", (c, s, i), g))
                    w = (p - 1) * 4 + i
                    bc, scale = (bias, 1.0) if i == G_ else (bias_half, 0.5)
                    act.activation(gate[:, c, i, 0:n], gate_bank(c, s, i), ACT.Tanh, bias=bc[:, w:w + 1],
                                   scale=scale).then_inc(S["gate_act"], 1)

            def cell_tanh(g, c, s):
                n = size(s)
                done = "input_done" if STEPS[s][1] == 0 else "cell_done"
                act.wait_ge(S[done], after(done, (c, s), g))
                act.activation(tanh_c[:, c, 0:n], cell[:, c, 0:n], ACT.Tanh, scale=0.5).then_inc(S["tanh_done"], 1)

            def high(kind):
                def go(g, q):
                    dst = x1t_hi[:, q % 2, :] if kind == "turn" else part[kind, "hi"][:, q, :]
                    act.wait_ge(S["mix_mm"], after("mix_mm", (kind, q), g))
                    act.activation(dst, mix_bank((kind, q), g), ACT.Copy).then_inc(S["hi_done"], 1)
                return go

            def value_high(g, q):
                act.wait_ge(S["mix_mm"], after("mix_mm", ("value", q), g))
                act.activation(value_hi[:, q, :, :, 0:HD],
                               mix_bank(("value", q), g).rearrange("p (b h d) -> p b h d", b=QB, h=HEADS),
                               ACT.Copy).then_inc(S["hi_done"], 1)

            def expo(g, q, b):
                act.wait_ge(S["expo_mm"], after("expo_mm", (q, b), g))
                act.activation(prob_t[:, b, :, :], expo_bank((q, b), g).rearrange("p (h t) -> p h t", h=HEADS), ACT.Exp,
                               scale=HD ** -0.5).then_inc(S["expo_done"], 1)

            def head(g_graph, g_cell):
                if g_graph is not None:
                    for q in range(NQ):
                        if not isinstance(g_graph, int) or g_graph > 0:
                            act.wait_ge(S["graph_mm"], after("graph_mm", (q, 0), g_graph - 1))
                        act.dma_start(x_in[:, q, :, :], x_quads[g_graph, q]).then_inc(x_in_done[q], 16)

            act.wait_ge(prep_dve, PREP_DVE)
            run(act, {"head": head, "graph": graph, "cell_mm": gates, "cell_tanh": cell_tanh,
                      "turn": high("turn"),
                      "query": high("query"), "key": high("key"), "value": value_high,
                      "expo": expo})



        @block.vector
        def _(dve):
            owned(dve, ["graph_evac0", "graph_evac1", "input_done", "forget_done", "cell_done", "hidden_done", "hidden_hi", "hidden_lo", "y_done", "stats_done1", "stats_done2",
                        "x1_done", "out_done", "mix_evac", "max_done", "shift_hi", "shift_lo",
                        "recip_done"])
            dve.wait_ge(weights_in, 16 * 10)
            dve.tensor_tensor(b_sum[:], b_raw[:, 0, :], b_raw[:, 1, :], ALU.add).then_inc(prep_dve, 1)
            dve.tensor_scalar(mask[:], adj_sb[:], 0.0, MASKED, ALU.is_equal, ALU.mult).then_inc(prep_dve, 1)
            dve.wait_ge(prep_mm, 1)
            dve.tensor_scalar(mask_t[:], ps_score[:, 0, :], 0.0, MASKED, ALU.is_equal,
                              ALU.mult).then_inc(prep_dve, 1)
            dve.tensor_copy(adj_t[:], ps_score[:, 0, :]).then_inc(prep_dve, 1)
            dve.tensor_copy(bg_all[:], ps_score[:, 2:4, :]).then_inc(prep_dve, 1)
            dve.wait_ge(prep_mm, 2)
            dve.tensor_copy(bias[:], ps_expo[:, 0, 0:NW]).then_inc(prep_dve, 1)
            dve.tensor_scalar(bias_half[:], ps_expo[:, 0, 0:NW], 0.5, None, ALU.mult).then_inc(prep_dve, 1)
            for n in range(2 * NW // 4):
                dve.wait_ge(prep_act, n + 1)
                dve.scalar_tensor_tensor(out=w_lo[:, 4 * n:4 * n + 4, :],
                                         in0=ps_gate[:, n % GATE_BANKS, :].rearrange("p (c d) -> p c d", c=4),
                                         scalar=1.0 if n == 0 else 0.5, in1=w_hi[:, 4 * n:4 * n + 4, :],
                                         op0=ALU.mult, op1=ALU.subtract).then_inc(prep_dve, 1)
            dve.wait_ge(prep_act, 2 * NW // 4 + 1)
            dve.tensor_tensor(wqkv_lo[:], wqkv_sb[:], wqkv_hi[:], ALU.subtract).then_inc(prep_dve, 1)
            dve.wait_ge(prep_dve, PREP_DVE)

            def graph(g, q, k):
                src = graph_bank(q, g).rearrange("p (b t) -> p b t", b=QB)
                if k in (1, 3):
                    dve.wait_ge(S["graph_mm"], after("graph_mm", (q, k), g))
                    dve.tensor_tensor(u[:, q % 2, :, :], src, bg_all[:, k // 2, None, :].to_broadcast([P, QB, D]),
                                      ALU.add).then_inc(S[f"graph_evac{q % 2}"], 1)
                elif k == 4:
                    dve.wait_ge(S[f"graph_evac{q % 2}"], after(f"graph_evac{q % 2}", (q, "hi"), g))
                    dve.scalar_tensor_tensor(out=quad(h2_lo, q), in0=src, scalar=0.0, in1=quad(h2_hi, q),
                                             op0=ALU.max, op1=ALU.subtract).then_inc(S[f"graph_evac{q % 2}"], 1)

            def new_cell(g, c, s):
                n = size(s)
                late = STEPS[s][1] > 0
                dve.wait_ge(S["gate_act"], after("gate_act", (c, s, G_), g))
                dve.scalar_tensor_tensor(out=(inp if late else cell)[:, c, 0:n], in0=gate[:, c, I_, 0:n], scalar=1.0,
                                         in1=gate[:, c, G_, 0:n], op0=ALU.add,
                                         op1=ALU.mult).then_inc(S["input_done"], 1)
                if late:
                    dve.wait_ge(S["gate_act"], after("gate_act", (c, s, F_), g))
                    dve.scalar_tensor_tensor(out=forget[:, c, 0:n], in0=gate[:, c, F_, 0:n], scalar=1.0,
                                             in1=cell[:, c, 0:n], op0=ALU.add,
                                             op1=ALU.mult).then_inc(S["forget_done"], 1)
                    dve.wait_ge(S["forget_done"], after("forget_done", (c, s), g))
                    dve.scalar_tensor_tensor(out=cell[:, c, 0:n], in0=forget[:, c, 0:n], scalar=0.5,
                                             in1=inp[:, c, 0:n], op0=ALU.mult,
                                             op1=ALU.add).then_inc(S["cell_done"], 1)

            def cell_end(g, c, s):
                n = size(s)
                dve.wait_ge(S["tanh_done"], after("tanh_done", (c, s), g))
                dve.scalar_tensor_tensor(out=hidden[:, c, 0:n], in0=gate[:, c, O_, 0:n], scalar=1.0,
                                         in1=tanh_c[:, c, 0:n], op0=ALU.add,
                                         op1=ALU.mult).then_inc(S["hidden_done"], 1)
                ends = ends_window(s)
                hi = columns(state_hi, c, s) if ends else dense(run_hi[:, c, :], s)
                lo = columns(state_lo, c, s) if ends else dense(run_lo[:, c, :], s)
                dve.wait_ge(S["hidden_done"], after("hidden_done", (c, s), g))
                dve.tensor_copy(hi, dense(hidden[:, c, :], s)).then_inc(S["hidden_hi"], 1)
                dve.wait_ge(S["hidden_hi"], after("hidden_hi", (c, s), g))
                dve.tensor_tensor(lo, dense(hidden[:, c, :], s), hi, ALU.subtract).then_inc(S["hidden_lo"], 1)

            def cell_out(g, q):
                dve.wait_ge(x_res_done[q], g * 16 + 16)
                dve.wait_ge(S["turned_mm"], after("turned_mm", q, g))
                dve.scalar_tensor_tensor(out=quad(y, q), in0=ps_gate[:, q % GATE_BANKS, :].rearrange("p (b d) -> p b d", b=QB),
                                         scalar=0.5, in1=quad(y, q), op0=ALU.mult,
                                         op1=ALU.add).then_inc(S["y_done"], 1)

            def moments_of(n):
                def go(g, q):
                    i = int(n) - 1
                    src, at = (y, q) if n == "1" else (z, q % 2)
                    if n == "1":
                        dve.wait_ge(S["y_done"], after("y_done", q, g))
                    else:
                        dve.wait_ge(S["z_done"], after("z_done", (q, 1), g))
                    for b in range(QB):
                        ins = dve.bn_stats(stats[:, i, q * QB + b, :], src[:, at * QB + b, :])
                    ins.then_inc(S["stats_done" + n], 1)
                return go

            def normalise(n):
                def go(g, q):
                    i = int(n) - 1
                    src, dst, at, done = (y, x1, q, "x1_done") if n == "1" else (z, result, q % 2, "out_done")
                    dve.wait_ge(S["rstd_done" + n], after("rstd_done" + n, q, g))
                    if n == "2":
                        dve.wait_ge(out_stored[q % 2], (g * (NQ // 2) + q // 2 + 1) * 16)
                    elif not (isinstance(g, int) and g == 0):
                        dve.wait_ge(S["z_done"], before("z_done", order_of("z_done", g)[0], g))
                    for b in range(QB):
                        r = q * QB + b
                        ins = dve.tensor_scalar(dst[:, at * QB + b, :], src[:, at * QB + b, :], mean[:, i, r:r + 1],
                                                rstd[:, i, r:r + 1], ALU.subtract, ALU.mult)
                    ins.then_inc(S[done], 1)
                return go

            def low(kind):
                def go(g, q):
                    hi, lo = ((x1t_hi[:, q % 2, :], x1t_lo[:, q % 2, :]) if kind == "turn"
                              else (part[kind, "hi"][:, q, :], part[kind, "lo"][:, q, :]))
                    dve.wait_ge(S["hi_done"], after("hi_done", (kind, q), g))
                    dve.tensor_tensor(lo, mix_bank((kind, q), g), hi, ALU.subtract).then_inc(S["mix_evac"], 1)
                return go

            def value_low(g, q):
                dve.wait_ge(S["hi_done"], after("hi_done", ("value", q), g))
                dve.tensor_tensor(value_lo[:, q, :, :, 0:HD],
                                  mix_bank(("value", q), g).rearrange("p (b h d) -> p b h d", b=QB, h=HEADS),
                                  value_hi[:, q, :, :, 0:HD], ALU.subtract).then_inc(S["mix_evac"], 1)

            def row_maxima(g, q, b):
                dve.wait_ge(S["score_mm"], after("score_mm", (q, b), g))
                dve.tensor_reduce(row_max[:, q, b * HEADS:(b + 1) * HEADS],
                                  score_bank((q, b), g).rearrange("p (h t) -> p h t", h=HEADS), AX_X,
                                  ALU.max).then_inc(S["max_done"], 1)

            def shift(g, q):
                n = QB * HEADS
                dve.wait_ge(S["max_done"], after("max_done", (q, QB - 1), g))
                dve.tensor_scalar(shift_parts[:, q, 0:n], row_max[:, q, :], -1.0, None,
                                  ALU.mult).then_inc(S["shift_hi"], 1)
                dve.wait_ge(S["shift_hi"], after("shift_hi", q, g))
                dve.scalar_tensor_tensor(out=shift_parts[:, q, n:2 * n], in0=row_max[:, q, :], scalar=-1.0,
                                         in1=shift_parts[:, q, 0:n], op0=ALU.mult,
                                         op1=ALU.subtract).then_inc(S["shift_lo"], 1)
                dve.wait_ge(S["mix_mm"], after("mix_mm", ("shift", q), g))
                dve.tensor_copy(shift_t[:, q, :],
                                mix_bank(("shift", q), g).bitcast(BF16)[0:2 * n, 0:P]).then_inc(S["mix_evac"], 1)

            def mix(g, q, m):
                heads = mix_bank((q, m), g)[:, 0:2 * HEADS * VW].rearrange("p (n v) -> p n v", v=VW)
                dve.wait_ge(S["mix_mm"], after("mix_mm", (q, m), g))
                dve.reciprocal(recip[:, m, :], heads[:, :, HD]).then_inc(S["recip_done"], 1)
                dve.wait_ge(S["recip_done"], after("recip_done", (q, m), g))
                dve.wait_ge(S["z_done"], before("z_done", (q, m), g))
                dve.tensor_tensor(mixed[:, m, :, :], heads[:, :, 0:HD],
                                  recip[:, m, :, None].to_broadcast([P, 2 * HEADS, HD]),
                                  ALU.mult).then_inc(S["mix_evac"], 1)

            run(dve, {"graph": graph, "cell_mm": new_cell, "cell_end": cell_end,
                      "cell_out": cell_out, "stat1": moments_of("1"), "norm1": normalise("1"), "turn": low("turn"), "query": low("query"),
                      "key": low("key"), "value": value_low, "score": row_maxima, "shift": shift, "mix": mix,
                      "stat2": moments_of("2"), "out": normalise("2")})


INPUTS = ["x", "adj", "L0_gnn_Wg0", "L0_gnn_bg0", "L0_gnn_Wg1", "L0_gnn_bg1", "L0_gnn_Wih", "L0_gnn_Whh",
          "L0_gnn_bih", "L0_gnn_bhh", "L1_gnn_W"]


def kernel(**inputs):
    import concourse.bacc as bacc
    from concourse.bass_utils import run_bass_kernel_spmd

    nc = bacc.Bacc("TRN2", target_bir_lowering=False, num_devices=1)
    arrays, args = {}, []
    for name in INPUTS:
        a = np.ascontiguousarray(inputs[name])
        arrays[f"in_{name}"] = a
        args.append(nc.dram_tensor(f"in_{name}", a.shape, mybir.dt.from_np(a.dtype), kind="ExternalInput").ap())
    args.append(nc.dram_tensor("out_0", (B, T, D), F32, kind="ExternalOutput").ap())
    build(nc, *args)
    r = run_bass_kernel_spmd(nc, [arrays], core_ids=[0])
    return r.results[0]["out_0"]
```

```python
from contextlib import ExitStack

import numpy as np

import concourse.bass as bass
from concourse import mybir

F32 = mybir.dt.float32
F16 = mybir.dt.float16
BF16 = mybir.dt.bfloat16
ALU = mybir.AluOpType
ACT = mybir.ActivationFunctionType
AX_X = mybir.AxisListType.X

P = 128
B, T, D = 128, 128, 128
GB = 16
QB = 4
NQ = GB // QB
NG = B // GB
W = QB * T
HEADS, HD = 4, 32
MAX_SKIP = 4
CHAINS = 2
CB = GB // CHAINS
EPS = 1e-5
MASKED = -1e30
SLOTS = 3
SHIFT_UNIT = 32768.0
STACK = SLOTS * HD + 2
VW = HD + 1
GATE_BANKS = 3
MIX_BANKS = 2
I_, F_, G_, O_ = range(4)

STEPS = [(1, 0, b, QB, T) for b in range(0, CB, QB)]
STEPS += [(p, t, 0, CB, T // p) for p in range(2, MAX_SKIP + 1) for t in range(p)]
LAST = len(STEPS) - 1
WEIGHT_LOADS = 2 * MAX_SKIP


def gates_of(s):
    return (I_, G_, O_) if STEPS[s][1] == 0 else (I_, G_, F_, O_)


HEAD, START, FULL, END, TAIL = range(5)
LAG = {"graph": 0, "cell": 1, "mix": 2}

PACE = {
    HEAD: {
        "graph": [(-9.23, 1.03), (-9.5, 0.99), (-6.0, 0.6), (-5.5, 1.0)],
        "weights": [(-10.0, 1.11)],
        "moved": {
            "graph 2 1": -0.06, "weights 7": -0.53, "graph 3 2": 0.45,
        },
    },
    START: {
        "graph": [(0.3, 2.07), (1.3, 2.0), (10.3, 2.18), (11.3, 2.0)],
        "tanh": [0.49, 0.37, 0.09, 0.61],
        "end": [0.57, 0.1, 0.398, 0.44],
        "turned": [21.0, 21.37, 21.448, 21.468],
        "stat": [21.418, 21.59, 21.62, 21.95],
        "chain0": [0.0, 2.0, 4.0, 6.0, 8.0, 10.0, 12.0, 14.0, 16.0, 18.0, 20.0],
        "chain1": [1.0, 3.0, 5.0, 7.0, 9.0, 11.0, 13.0, 15.0, 17.0, 19.0, 21.0],
        "moved": {
            "graph 3 3": 2.75, "cell_mm 0 5": 0.01, "graph 2 1": -0.12, "graph 1 3": 0.17,
            "graph 3 0": -1.55, "cell_end 1 10": -0.29, "stat1 3": -0.02,
        },
    },
    FULL: {
        "first": [(0.0, 0.57), (5.54, 0.54)],
        "attend": [(8.2, 0.5, 0.99), (11.1, 0.49, 0.8), (13.01, 0.51, 0.8), (15.05, 0.47, 0.8)],
        "graph": [(0.3, 2.08), (1.3, 2.22), (10.45, 2.06), (11.29, 1.48)],
        "tanh": [0.484, 0.2, 0.37, 0.35],
        "end": [0.29, 0.32, 0.48, 0.44],
        "turned": [21.68, 21.69, 21.72, 21.74],
        "stat": [21.76, 23.15, 25.52, 23.15],
        "chain0": [0.0, 2.0, 4.0, 6.0, 8.0, 10.0, 12.0, 14.0, 16.0, 18.0, 20.0],
        "chain1": [1.0, 3.0, 5.0, 7.0, 9.0, 11.0, 13.0, 15.0, 17.0, 19.0, 21.0],
        "moved": {
            "cell_mm 1 7": -0.76, "cell_mm 1 3": -0.26, "graph 0 0": -1.02, "graph 3 2": 0.87,
            "shift 0": 0.02, "cell_mm 0 8": -0.33, "score 1 1": 0.06, "expo 1 3": -0.29,
            "cell_mm 0 1": -0.08, "cell_end 0 7": 0.28, "cell_tanh 0 5": -0.01, "graph 3 1": 0.6,
            "cell_end 1 9": 0.62,
        },
    },
    END: {
        "first": [(0.0, 0.57), (5.54, 0.54)],
        "attend": [(8.2, 0.5, 0.99), (11.1, 0.49, 0.8), (13.01, 0.51, 0.8), (15.05, 0.47, 0.8)],
        "tanh": [0.484, 0.2, 0.37, 0.35],
        "end": [0.29, 0.32, 0.48, 0.44],
        "turned": [21.68, 21.69, 21.72, 21.74],
        "stat": [21.76, 23.15, 25.52, 23.15],
        "chain0": [0.0, 2.0, 4.0, 6.0, 8.0, 10.22, 12.0, 14.0, 16.0, 18.0, 20.0],
        "chain1": [1.0, 3.0, 5.0, 7.0, 9.0, 11.0, 13.0, 15.0, 17.0, 19.0, 21.0],
        "moved": {
            "score 1 3": 0.18, "score 1 1": -0.08, "cell_mm 0 2": -0.09,
        },
    },
    TAIL: {
        "first": [(26.5, 0.25), (29.87, 0.1)],
        "attend": [(32.75, 0.56, 1.0), (35.22, 0.58, 1.0), (38.12, 0.55, 1.0), (40.55, 0.52, 1.0)],
        "moved": {
            "out 1": 0.98, "key 3": 0.05, "value 3": -0.4, "expo 3 1": -0.08, "mix 1 1": 0.36,
            "stat2 0": -0.06, "out 0": 0.78, "expo 1 3": -0.93,
        },
    },
}


def pieces_of(pace):
    timed = []
    if "tanh" in pace:
        for c in range(CHAINS):
            for s, time in enumerate(pace[f"chain{c}"]):
                p = STEPS[s][0]
                timed += [(time, ("cell_mm", c, s)), (time + pace["tanh"][p - 1], ("cell_tanh", c, s)),
                          (time + pace["end"][p - 1], ("cell_end", c, s))]
        for q in range(NQ):
            timed += [(pace["turned"][q], ("cell_out", q)), (pace["stat"][q], ("stat1", q))]
    for i, (start, step) in enumerate(pace.get("first", [])):
        pieces = [(kind, q) for kind in ("norm1", "turn", "query", "key", "value") for q in (2 * i, 2 * i + 1)]
        timed += [(start + k * step, piece) for k, piece in enumerate(pieces)]
    for q, (start, step, placing) in enumerate(pace.get("attend", [])):
        pieces = [("score", q, b) for b in range(QB)] + [("parts", q), ("shift", q), ("expo", q, 0)]
        pieces += [("expo", q, 1), ("expo", q, 2), ("mix", q, 0), ("expo", q, 3), ("mix", q, 1)]
        pieces += [("stat2", q), ("out", q)]
        placed = pieces.index(("shift", q))
        timed += [(start + k * step + placing * (k > placed), piece) for k, piece in enumerate(pieces)]
    for q, (start, step) in enumerate(pace.get("graph", [])):
        timed += [(start + k * step, ("graph", q, k)) for k in range(4)]
    for start, step in pace.get("weights", []):
        timed += [(start + n * step, ("weights", n)) for n in range(WEIGHT_LOADS)]
    moved = pace.get("moved", {})
    return [(time + moved.get(" ".join(map(str, piece)), 0.0), piece) for time, piece in timed]


def plan(*kinds):
    timed = [(time, kind, piece) for kind in kinds for time, piece in pieces_of(PACE[kind])]
    order = [(kind, piece) for _, kind, piece in sorted(timed, key=lambda item: item[0])]
    at = {item: i for i, item in enumerate(order)}
    for kind in kinds:
        if "tanh" in PACE[kind]:
            for q in range(NQ):
                c = q * QB // CB
                assert at[kind, ("stat1", q)] > at[kind, ("cell_out", q)] > at[kind, ("cell_end", c, LAST)]
                assert (kind == END and c == 0) or at[kind, ("cell_out", q)] > at[kind, ("cell_mm", CHAINS - 1, LAST)]
                assert q == 0 or at[kind, ("cell_out", q)] > at[kind, ("cell_out", q - 1)]
            assert at[kind, ("cell_mm", 0, 0)] < at[kind, ("cell_mm", 1, 0)]
            assert at[kind, ("cell_end", 0, LAST)] < at[kind, ("cell_end", 1, LAST)]
            assert kind == END or at[kind, ("cell_end", 0, LAST)] > at[kind, ("cell_end", 1, LAST - 1)]
        if "attend" in PACE[kind]:
            for q in range(NQ):
                for name, count in (("score", QB), ("expo", QB), ("mix", QB // 2)):
                    assert all(at[kind, (name, q, n - 1)] < at[kind, (name, q, n)] for n in range(1, count))
                assert at[kind, ("score", q, QB - 1)] < at[kind, ("parts", q)] < at[kind, ("shift", q)]
                assert all(at[kind, ("expo", q, 2 * m + 1)] < at[kind, ("mix", q, m)] for m in range(QB // 2))
                assert at[kind, ("mix", q, 1)] < at[kind, ("stat2", q)] < at[kind, ("out", q)]
            for q in range(1, NQ):
                assert all(at[kind, ("expo", q, b)] > at[kind, ("mix", q - 1, b // 2)] for b in range(QB))
            for q in range(2, NQ):
                assert at[kind, ("mix", q, 0)] > at[kind, ("out", q - 2)]
                assert at[kind, ("turn", q)] > at[kind, ("value", q - 2)]
        if "graph" in PACE[kind]:
            for q in range(2, NQ):
                assert at[kind, ("graph", q, 0)] > at[kind, ("graph", q - 2, 3)]
            if "tanh" in PACE[kind]:
                per_chain = CB // QB
                assert all(at[kind, ("graph", q, 3)] > at[kind, ("cell_mm", q // per_chain, q % per_chain)]
                           for q in range(NQ))
    if END in kinds and TAIL in kinds:
        assert at[TAIL, ("norm1", 0)] > at[END, ("mix", NQ - 1, 1)]
        assert all(at[TAIL, ("mix", q, 0)] > at[END, ("out", q + 2)] for q in range(2))
    return order


OPENING, LOOP, CLOSING = plan(HEAD, START), plan(FULL), plan(END, TAIL)

STREAM = {"cell_mm": "cell", "cell_out": "cell", "cell_tanh": "cell", "cell_end": "cell", "stat1": "cell",
          "graph": "graph", "weights": "graph"}


def signals(piece):
    kind = piece[0]
    if kind == "graph":
        _, q, k = piece
        evac = ["hi", "lo"] if k == 3 else [k]
        return [("graph_mm", (q, k))] + [(f"graph_evac{q % 2}", (q, e)) for e in evac]
    if kind == "cell_mm":
        key = piece[1:]
        late = STEPS[key[1]][1] > 0
        out = [(n, (*key, c)) for c in gates_of(key[1]) for n in ("gate_mm", "gate_act")]
        return out + [("input_done", key)] + [("forget_done", key)] * late + [("cell_done", key)] * late
    if kind == "weights":
        return []
    if kind == "cell_tanh":
        return [("tanh_done", piece[1:])]
    if kind == "cell_end":
        return [(n, piece[1:]) for n in ("hidden_done", "hidden_hi", "hidden_lo")]
    if kind == "cell_out":
        return [(n, piece[1]) for n in ("turned_mm", "y_done")]
    if kind in ("stat1", "stat2"):
        n = kind[-1]
        names = ("stats_done", "pair_done", "half_done", "square_done", "eps_done", "rstd_done")
        return [(name + n, piece[1]) for name in names]
    if kind == "norm1":
        return [("x1_done", piece[1])]
    if kind == "out":
        return [("out_done", piece[1])]
    q = piece[1]
    if kind in ("turn", "query", "key", "value"):
        return [("mix_mm", (kind, q)), ("hi_done", (kind, q)), ("mix_evac", (kind, q))]
    if kind == "score":
        return [("score_mm", (q, piece[2])), ("max_done", (q, piece[2]))]
    if kind == "parts":
        return [("shift_hi", q), ("shift_lo", q)]
    if kind == "shift":
        return [("mix_mm", (kind, q)), ("mix_evac", (kind, q))]
    if kind == "expo":
        return [("expo_mm", (q, piece[2])), ("expo_done", (q, piece[2])), ("prob_lo_done", (q, piece[2]))]
    if kind == "mix":
        key = (q, piece[2])
        return [("mix_mm", key), ("recip_done", key), ("mix_evac", key), ("z_done", key)]
    raise ValueError(kind)


def stream_of(piece):
    return STREAM.get(piece[0], "mix")


ORDER, STREAM_OF, RUNS = {}, {}, {}
for _kind, _piece in OPENING + LOOP + CLOSING:
    for _sem, _key in signals(_piece):
        ORDER.setdefault((_sem, _kind), []).append(_key)
        STREAM_OF[_sem] = stream_of(_piece)
        if RUNS.setdefault(_sem, [_kind])[-1] != _kind:
            RUNS[_sem].append(_kind)
assert all(runs == sorted(set(runs)) for runs in RUNS.values())
COUNT = {sem: len(ORDER[sem, FULL]) for sem in STREAM_OF}
assert COUNT["gate_mm"] % GATE_BANKS == 0 and COUNT["mix_mm"] % MIX_BANKS == 0


def order_of(sem, g):
    if not isinstance(g, int):
        return ORDER[sem, FULL]
    r = g + LAG[STREAM_OF[sem]]
    return ORDER[sem, HEAD if r == 0 else START if r == 1 else FULL if r < NG else END if r == NG else TAIL]


def after(sem, key, g):
    return g * COUNT[sem] + (order_of(sem, g).index(key) + 2)


def before(sem, key, g):
    return g * COUNT[sem] + (order_of(sem, g).index(key) + 1)


_CELL_END = CLOSING.index((END, ("cell_out", NQ - 1)))
EARLY = {_sem: sum(kind == TAIL and _sem in dict(signals(piece)) for kind, piece in CLOSING[:_CELL_END])
         for _sem in ("mix_mm", "score_mm", "expo_mm")}


def bank_of(sem, banks, key, g):
    n = order_of(sem, g).index(key)
    if not isinstance(g, int) or g < NG - 1 or n < EARLY[sem]:
        return n % banks, n - banks
    turn, extra = n - EARLY[sem], 1
    place = turn % (banks + extra)
    if turn < extra:
        return banks, None
    if turn < banks + extra:
        return (EARLY[sem] + place - extra) % banks, EARLY[sem] + place - extra - banks
    return (banks if place < extra else (EARLY[sem] + place - extra) % banks), n - banks - extra


def build(nc, x, adj, wg0, bg0, wg1, bg1, wih, whh, bih, bhh, wqkv, out):
    ctx = ExitStack()
    with ctx:
        def sb(name, shape, dt):
            return ctx.enter_context(nc.sbuf_tensor(name, shape, dt))

        def pb(name, shape, dt):
            return ctx.enter_context(nc.psum_tensor(name, shape, dt))

        def sem(name):
            return ctx.enter_context(nc.semaphore(name))

        ident = sb("ident", [P, P], F32)
        ident16 = sb("ident16", [P, P], F16)
        identb = sb("identb", [P, P], BF16)
        minus_half = sb("minus_half", [P, QB], F32)
        half = sb("half", [P, QB], F32)
        adj_sb = sb("adj_sb", [P, T], F32)
        adj_t = sb("adj_t", [P, T], F32)
        place = sb("place", [1, 2, 3, 9], BF16)
        bias_rows = sb("bias_rows", [9, 3, D], BF16)
        ones_col = sb("ones_col", [P, 1], F32)
        mask = sb("mask", [P, T], BF16)
        mask_t = sb("mask_t", [P, T], BF16)
        wg = sb("wg", [P, 2, D], F32)
        NW = MAX_SKIP * 4
        w_hi = sb("w_hi", [P, 2 * NW, D], F16)
        w_lo = sb("w_lo", [P, 2 * NW, D], F16)
        b_raw = sb("b_raw", [NW, 2, D], F32)
        b_sum = sb("b_sum", [NW, D], F32)
        bias = sb("bias", [P, NW], F32)
        bias_half = sb("bias_half", [P, NW], F32)
        wqkv_sb = sb("wqkv_sb", [P, 3 * D], F32)
        wqkv_hi = sb("wqkv_hi", [P, 3 * D], F16)
        wqkv_lo = sb("wqkv_lo", [P, 3 * D], F16)
        x_in = sb("x_in", [P, NQ, QB, D], F32)
        mixed_x = sb("mixed_x", [P, 2, QB, T], F32)
        h1 = sb("h1", [P, 2, QB, D], F32)
        mixed_h1 = sb("mixed_h1", [P, 2, QB, T], F32)
        h2_hi = sb("h2_hi", [P, GB, T], F16)
        h2_lo = sb("h2_lo", [P, GB, T], F16)
        state_hi = sb("state_hi", [P, GB, T], F16)
        state_lo = sb("state_lo", [P, GB, T], F16)
        run_hi = sb("run_hi", [P, CHAINS, W], F16)
        run_lo = sb("run_lo", [P, CHAINS, W], F16)
        gate = sb("gate", [P, CHAINS, 4, W], F32)
        gate_line = gate[0:1, :, :, :].rearrange("p c i w -> p (c i w)")
        rows = gate_line[:, 0:3 * D].rearrange("p (a d) -> p a d", a=3)
        rows_left = gate_line[:, 3 * D:6 * D].rearrange("p (a d) -> p a d", a=3)
        rows_part = gate_line.bitcast(BF16)[:, 12 * D:21 * D].rearrange("p (j a d) -> p j a d", j=3, a=3)
        inp = sb("inp", [P, CHAINS, W], F32)
        forget = sb("forget", [P, CHAINS, W], F32)
        cell = sb("cell", [P, CHAINS, W], F32)
        tanh_c = sb("tanh_c", [P, CHAINS, W], F32)
        hidden = sb("hidden", [P, CHAINS, W], F32)
        y = sb("y", [P, GB, D], F32)
        x1 = sb("x1", [P, GB, D], F32)
        stats = sb("stats", [P, 2, GB, 6], F32)
        mean_sum, mean_gap, squares, squares_eps, half_gap, gap_square, var_eps = (
            sb(n, [P, QB], F32)
            for n in ("mean_sum", "mean_gap", "squares", "squares_eps", "half_gap", "gap_square", "var_eps"))
        mean = sb("mean", [P, 2, GB], F32)
        rstd = sb("rstd", [P, 2, GB], F32)
        x1t_hi = sb("x1t_hi", [P, 2, W], F16)
        x1t_lo = sb("x1t_lo", [P, 2, W], F16)
        part = {(n, h): sb(f"{n}_{h}", [P, NQ, W], F16) for n in ("query", "key") for h in ("hi", "lo")}
        query_stack = sb("query_stack", [P, 2, 2, HEADS, W], F16)
        w_raw = query_stack[:].rearrange("p a b h w -> p (a b h w)").bitcast(F32).rearrange("p (n d) -> p n d", d=D)
        key_stack = sb("key_stack", [P, 2, 2, HEADS, W], F16)
        value_hi = sb("value_hi", [P, NQ, QB, HEADS, VW], F16)
        value_lo = sb("value_lo", [P, NQ, QB, HEADS, VW], F16)
        row_max = sb("row_max", [P, NQ, QB * HEADS], F32)
        shift_parts = sb("shift_parts", [P, NQ, 2 * QB * HEADS], F16)
        shift_t = sb("shift_t", [2 * QB * HEADS, NQ, P], F16)
        prob_t = sb("prob_t", [P, QB, HEADS, T], F32)
        prob_hi = prob_t[:].bitcast(BF16).rearrange("p b h (t two) -> p b h t two", two=2)[:, :, :, :, 1]
        prob_lo = sb("prob_lo", [P, QB, HEADS, T], F16)
        recip = sb("recip", [P, 2, 2 * HEADS], F32)
        mixed = sb("mixed", [P, 2, 2 * HEADS, HD], F32)
        z = sb("z", [P, 2 * QB, D], F32)
        result = sb("result", [P, 2 * QB, D], F32)

        ps_gate = pb("ps_gate", [P, GATE_BANKS, W], F32)
        ps_score = pb("ps_score", [P, HEADS, T], F32)
        ps_expo = pb("ps_expo", [P, HEADS, T], F32)
        ps_mix = pb("ps_mix", [P, MIX_BANKS, W], F32)
        ps_graph = pb("ps_graph", [P, W], F32)

        S = {name: sem(name) for name in STREAM_OF}
        small_in = sem("small_in")
        lstm_in = [sem(f"lstm_in{n}") for n in range(WEIGHT_LOADS)]
        consts_done = sem("consts_done")
        prep_mm = sem("prep_mm")
        weights_mm = sem("weights_mm")
        weights_hi = sem("weights_hi")
        split_done = sem("split_done")
        wqkv_split = sem("wqkv_split")
        prep_dve = sem("prep_dve")
        rows_done = sem("rows_done")
        x_in_done = [sem(f"x_in_done{q}") for q in range(NQ)]
        x_res_done = [sem(f"x_res_done{q}") for q in range(NQ)]
        stack_done = [sem(f"stack_done{pair}") for pair in range(NQ // 2)]
        shift_placed = [sem(f"shift_placed{q}") for q in range(NQ)]
        out_stored = [sem(f"out_stored{r}") for r in range(2)]

        x_quads = x.rearrange("(g q b) t d -> g q t b d", g=NG, q=NQ)
        out_quads = out.rearrange("(g q b) t d -> g q t b d", g=NG, q=NQ)

        def quad(buf, q):
            return buf[:, q * QB:(q + 1) * QB, :]

        def columns(buf, c, s):
            p, t, b0, nb, nw = STEPS[s]
            return buf[:, c * CB + b0:c * CB + b0 + nb, t:(nw - 1) * p + t + 1:p]

        def gate_bank(g, c, s, i):
            return ps_gate[:, order_of("gate_mm", g).index((c, s, i)) % GATE_BANKS, 0:size(s)]

        def mix_bank(key, g):
            return [ps_mix[:, 0, :], ps_mix[:, 1, :], ps_graph[:]][bank_of("mix_mm", MIX_BANKS, key, g)[0]]

        def score_bank(key, g):
            return [flat(ps_score), ps_gate[:, 0, :]][bank_of("score_mm", 1, key, g)[0]]

        def expo_bank(key, g):
            return [flat(ps_expo), ps_gate[:, 1, :]][bank_of("expo_mm", 1, key, g)[0]]

        def in_graph_bank(g, q):
            return isinstance(g, int) and g == NG - 1 and q < CB // QB

        def turned_bank(g, q):
            return ps_graph[:] if in_graph_bank(g, q) else ps_gate[:, q % GATE_BANKS, :]

        def graph_bank(q, g):
            return flat(ps_score) if isinstance(g, int) and g == 0 and q % 2 else ps_graph[:]

        def flat(bank):
            return bank[:].rearrange("p h t -> p (h t)")

        def size(s):
            return STEPS[s][3] * STEPS[s][4]

        def dense(buf, s):
            return buf[:, 0:size(s)].rearrange("p (b w) -> p b w", b=STEPS[s][3])

        def ends_window(s):
            return STEPS[s][1] == STEPS[s][0] - 1

        def owned(eng, names):
            for n in names:
                eng.sem_inc(S[n], 1)

        def run(eng, stages):
            def pieces(plan_, groups):
                for kind, piece in plan_:
                    if piece[0] in stages:
                        stages[piece[0]](groups[kind, stream_of(piece)], *piece[1:])
            if "load" in stages:
                stages["load"](0)
            pieces(OPENING, {(HEAD, "graph"): 0, (START, "graph"): 1, (START, "cell"): 0})
            with eng.Fori(1, NG - 1) as g:
                if "load" in stages:
                    stages["load"](g + 1)
                pieces(LOOP, {(FULL, "graph"): g + 1, (FULL, "cell"): g, (FULL, "mix"): g - 1})
            pieces(CLOSING, {(END, "cell"): NG - 1, (END, "mix"): NG - 2, (TAIL, "mix"): NG - 1})

        SMALL = 8
        CONSTS = 7 + 1 + 2 + 6
        PREP_DVE = 11
        block = ctx.enter_context(nc.Block())

        @block.sync
        def _(sp):
            for r in range(2):
                sp.sem_inc(out_stored[r], 16)
            sp.dma_start(adj_sb[:], adj).then_inc(small_in, 16)
            sp.dma_start(wg[:, 0, :], wg0).then_inc(small_in, 16)
            sp.dma_start(wg[:, 1, :], wg1).then_inc(small_in, 16)
            sp.dma_start(rows[:, 1, :], bg0.rearrange("(a d) -> a d", a=1)).then_inc(small_in, 16)
            sp.dma_start(rows[:, 2, :], bg1.rearrange("(a d) -> a d", a=1)).then_inc(small_in, 16)
            sp.dma_start(b_raw[:, 0, :], bih.rearrange("p (c d) -> (p c) d", c=4)).then_inc(small_in, 16)
            sp.dma_start(b_raw[:, 1, :], bhh.rearrange("p (c d) -> (p c) d", c=4)).then_inc(small_in, 16)
            sp.dma_start(wqkv_sb[:], wqkv).then_inc(small_in, 16)
            for n in range(WEIGHT_LOADS):
                w, p = (wih, whh)[n // MAX_SKIP], n % MAX_SKIP
                sp.dma_start(w_raw[:, 4 * n:4 * n + 4, :],
                             w[p].rearrange("(c r) d -> r c d", c=4)).then_inc(lstm_in[n], 16)

            for q in range(NQ):
                sp.dma_start(quad(y, q), x_quads[0, q]).then_inc(x_res_done[q], 16)

            def norm1(g, q):
                sp.wait_ge(S["x1_done"], after("x1_done", q, g))
                if not isinstance(g, int) or g < NG - 1:
                    sp.dma_start(quad(y, q), x_quads[g + 1, q]).then_inc(x_res_done[q], 16)

            def stack(kind):
                dst_all = query_stack if kind == "query" else key_stack
                halves = ("hi", "hi", "lo") if kind == "query" else ("hi", "lo", "hi")

                def go(g, q):
                    if q % 2 == 0:
                        return
                    sp.wait_ge(S["mix_evac"], after("mix_evac", (kind, q), g))
                    for slot, half in enumerate(halves):
                        for h in range(HEADS):
                            sp.dma_start(dst_all[slot * HD:(slot + 1) * HD, q // 2, :, h, :],
                                         part[kind, half][h * HD:(h + 1) * HD, q - 1:q + 1, :]
                                         ).then_inc(stack_done[q // 2], 16)
                return go

            def place_shift(g, q):
                sp.wait_ge(S["mix_evac"], after("mix_evac", ("shift", q), g))
                for half in range(2):
                    row = SLOTS * HD + half
                    sp.dma_start(query_stack[row:row + 1, q // 2, q % 2, :, :],
                                 shift_t[half * QB * HEADS:(half + 1) * QB * HEADS, q, :]).then_inc(shift_placed[q], 16)

            def store(g, q):
                sp.wait_ge(S["out_done"], after("out_done", q, g))
                sp.dma_start(out_quads[g, q], quad(result, q % 2)).then_inc(out_stored[q % 2], 16)

            run(sp, {"norm1": norm1, "query": stack("query"), "key": stack("key"), "shift": place_shift, "out": store})
            for r in range(2):
                sp.wait_ge(out_stored[r], 16 * (NG * NQ // 2 + 1))

        @block.gpsimd
        def _(pool):
            owned(pool, ["prob_lo_done", "z_done"])
            owned(pool, [name + n for n in "12" for name in ("pair_done", "half_done", "square_done", "eps_done",
                                                             "rstd_done")])
            pool.memset(ident[:], 0.0).then_inc(consts_done, 1)
            pool.memset(ones_col[:], 1.0).then_inc(consts_done, 1)
            pool.memset(minus_half[:], -0.5).then_inc(consts_done, 1)
            pool.memset(half[:], 0.5).then_inc(consts_done, 1)
            pool.memset(value_hi[:, :, :, :, HD:VW], 1.0).then_inc(consts_done, 1)
            pool.memset(value_lo[:, :, :, :, HD:VW], 0.0).then_inc(consts_done, 1)
            pool.memset(place[:], 0.0).then_inc(consts_done, 1)
            pool.wait_ge(consts_done, 7)
            pool.affine_select(out=ident[:], in_=ident[:], compare_op=ALU.not_equal, fill=1.0, base=0,
                               pattern=[[-1, P]], channel_multiplier=1).then_inc(consts_done, 1)
            pool.wait_ge(consts_done, 8)
            pool.tensor_copy(ident16[:], ident[:]).then_inc(consts_done, 1)
            pool.tensor_copy(identb[:], ident[:]).then_inc(consts_done, 1)
            for j in range(3):
                pool.memset(place[:, 0, j, j:9:3], 1.0).then_inc(consts_done, 1)
                pool.memset(place[:, 1, j, 3 * j:3 * j + 3], 1.0).then_inc(consts_done, 1)
            pool.wait_ge(consts_done, CONSTS)
            pool.memset(key_stack[SLOTS * HD:STACK, :, :, :, :], SHIFT_UNIT).then_inc(consts_done, 1)
            pool.wait_ge(consts_done, CONSTS + 1)

            def inverse_root(n):
                def go(g, q):
                    i = int(n) - 1
                    cut = slice(q * QB, (q + 1) * QB)
                    even, odd = (stats[:, i, cut, 3 * h:3 * h + 3] for h in range(2))
                    pool.wait_ge(S["stats_done" + n], after("stats_done" + n, q, g))
                    pool.tensor_tensor(mean_sum[:], even[:, :, 1], odd[:, :, 1], ALU.add)
                    pool.tensor_tensor(mean_gap[:], even[:, :, 1], odd[:, :, 1], ALU.subtract)
                    pool.tensor_tensor(squares[:], even[:, :, 2], odd[:, :, 2], ALU.add).then_inc(S["pair_done" + n], 1)
                    pool.wait_ge(S["pair_done" + n], after("pair_done" + n, q, g))
                    pool.tensor_tensor(mean[:, i, cut], mean_sum[:], half[:], ALU.mult)
                    pool.tensor_scalar(squares_eps[:], squares[:], 1.0 / D, EPS, ALU.mult, ALU.add)
                    pool.tensor_tensor(half_gap[:], mean_gap[:], half[:], ALU.mult).then_inc(S["half_done" + n], 1)
                    pool.wait_ge(S["half_done" + n], after("half_done" + n, q, g))
                    pool.tensor_tensor(gap_square[:], half_gap[:], half_gap[:],
                                       ALU.mult).then_inc(S["square_done" + n], 1)
                    pool.wait_ge(S["square_done" + n], after("square_done" + n, q, g))
                    pool.tensor_tensor(var_eps[:], squares_eps[:], gap_square[:],
                                       ALU.add).then_inc(S["eps_done" + n], 1)
                    pool.wait_ge(S["eps_done" + n], after("eps_done" + n, q, g))
                    pool.tensor_tensor(rstd[:, i, cut], var_eps[:], minus_half[:],
                                       ALU.pow).then_inc(S["rstd_done" + n], 1)
                return go

            def prob_low(g, q, b):
                pool.wait_ge(S["expo_done"], after("expo_done", (q, b), g))
                pool.tensor_tensor(prob_lo[:, b, :, :], prob_t[:, b, :, :], prob_hi[:, b, :, :],
                                   ALU.subtract).then_inc(S["prob_lo_done"], 1)

            def residual(g, q, m):
                pool.wait_ge(S["mix_evac"], after("mix_evac", (q, m), g))
                pool.tensor_tensor(z[:, (q % 2) * QB + 2 * m:(q % 2) * QB + 2 * m + 2, :],
                                   mixed[:, m, :, :].rearrange("p (b h) d -> p b (h d)", b=2),
                                   x1[:, q * QB + 2 * m:q * QB + 2 * m + 2, :], ALU.add).then_inc(S["z_done"], 1)

            run(pool, {"stat1": inverse_root("1"), "stat2": inverse_root("2"), "expo": prob_low,
                       "mix": residual})

        @block.tensor
        def _(pe):
            owned(pe, ["graph_mm", "gate_mm", "turned_mm", "mix_mm", "score_mm", "expo_mm"])
            pe.wait_ge(small_in, 16 * SMALL)
            pe.wait_ge(consts_done, CONSTS)
            pe.transpose(ps_score[:, 0, :], adj_sb[:], ident[:]).then_inc(prep_mm, 1)
            pe.wait_ge(prep_dve, 1)
            pe.transpose(ps_expo[:, 0, 0:NW], b_sum[:], ident[0:NW, 0:NW]).then_inc(prep_mm, 1)
            pe.wait_ge(prep_dve, 2)
            pe.matmul(ps_mix[0:1, 0, 0:T], ones_col[:], adj_t[:], start=True, stop=True).then_inc(prep_mm, 1)
            pe.wait_ge(prep_dve, 6)
            for j in range(3):
                pe.matmul(ps_mix[0:9, 1, 0:D], place[:, 0, j, :], rows_part[:, j, 0, :], start=j == 0, stop=j == 2)
            for j in range(3):
                mm = pe.matmul(ps_mix[0:9, 1, D:3 * D], place[:, 1, j, :], rows_part[:, j, 1:3, :],
                               start=j == 0, stop=j == 2)
            mm.then_inc(prep_mm, 1)
            pe.wait_ge(prep_dve, PREP_DVE)

            def weights(g, n):
                pe.wait_ge(lstm_in[n], 16)
                if n >= GATE_BANKS:
                    pe.wait_ge(split_done, n - GATE_BANKS + 1)
                for c in range(4):
                    mm = pe.transpose(ps_gate[:, n % GATE_BANKS, c * P:(c + 1) * P], w_raw[:, 4 * n + c, :], ident[:])
                mm.then_inc(weights_mm, 1)

            def three(out_, s_hi, s_lo, m_hi, m_lo):
                pe.matmul(out_, s_hi, m_hi, start=True, stop=False)
                pe.matmul(out_, s_lo, m_hi, start=False, stop=False)
                return pe.matmul(out_, s_hi, m_lo, start=False, stop=True)

            def graph(g, q, k):
                own = f"graph_evac{q % 2}"
                if k > 0:
                    pe.wait_ge(S[own], after(own, (q, k - 1), g))
                elif not (isinstance(g, int) and g == 0) or q >= 2:
                    pe.wait_ge(S[own], before(own, (q, 0), g))
                order = order_of("graph_mm", g)
                i = order.index((q, k))
                other = f"graph_evac{1 - q % 2}"
                if i == 0 and not (isinstance(g, int) and g == 0):
                    pe.wait_ge(S[other], before(other, order_of(other, g)[0], g))
                elif not (isinstance(g, int) and g == 0) and order[i - 1][0] % 2 != q % 2:
                    q_, k_ = order[i - 1]
                    pe.wait_ge(S[other], after(other, (q_, "lo" if k_ == 3 else k_), g))
                if k == 0:
                    pe.wait_ge(x_in_done[q], g * 16 + 16)
                if k in (1, 3):
                    sums, bg = bias_rows[:, 0, :], bias_rows[:, 1 + k // 2, :]
                    a, m = (sums, bg) if k == 1 else (bg, sums)
                    pe.matmul(graph_bank(q, g).rearrange("p (b t) -> p b t", b=QB), a,
                              m[:, None, :].to_broadcast([9, QB, T]), start=True, stop=False, skip_group_check=True)
                for b in range(QB):
                    o = graph_bank(q, g)[:, b * T:(b + 1) * T]
                    if k == 0:
                        mm = pe.matmul(o, x_in[:, q, b, :], adj_t[:], start=True, stop=True)
                    elif k == 1:
                        mm = pe.matmul(o, mixed_x[:, q % 2, b, :], wg[:, 0, :], start=False, stop=b == QB - 1,
                                       skip_group_check=True)
                    elif k == 2:
                        mm = pe.matmul(o, h1[:, q % 2, b, :], adj_t[:], start=True, stop=True)
                if k == 3:
                    mm = pe.matmul(graph_bank(q, g), wg[:, 1, :], mixed_h1[:, q % 2, :, :], start=False, stop=True,
                                   skip_group_check=True)
                mm.then_inc(S["graph_mm"], 1)

            def cell_mm(g, c, s):
                p, t, b0, nb, nw = STEPS[s]
                n = size(s)
                if p == 1:
                    q = (c * CB + b0) // QB
                    pe.wait_ge(S[f"graph_evac{q % 2}"], after(f"graph_evac{q % 2}", (q, "lo"), g))
                    if isinstance(g, int) and g == 0 and c == 0 and s == 0:
                        pe.wait_ge(split_done, WEIGHT_LOADS)
                    if c == 0 and s == 0:
                        pe.wait_ge(S["y_done"], before("y_done", 0, g))
                else:
                    pe.wait_ge(S["hidden_lo"], after("hidden_lo", (c, s - 1), g))
                src_hi, src_lo = (h2_hi, h2_lo) if p == 1 else (state_hi, state_lo)
                for i in gates_of(s):
                    w = (p - 1) * 4 + i
                    o = gate_bank(g, c, s, i)
                    last = order_of("gate_act", g).index((c, s, i)) - GATE_BANKS
                    if last >= 0 or not (isinstance(g, int) and g == 0):
                        pe.wait_ge(S["gate_act"], g * COUNT["gate_act"] + (last + 2))
                    pe.matmul(o, w_hi[:, w, :], columns(src_hi, c, s), start=True, stop=False)
                    pe.matmul(o, w_lo[:, w, :], columns(src_hi, c, s), start=False, stop=False)
                    mm = pe.matmul(o, w_hi[:, w, :], columns(src_lo, c, s), start=False, stop=t == 0)
                    if t > 0:
                        w += NW
                        pe.matmul(o, w_hi[:, w, :], run_hi[:, c, 0:n], start=False, stop=False)
                        pe.matmul(o, w_lo[:, w, :], run_hi[:, c, 0:n], start=False, stop=False)
                        mm = pe.matmul(o, w_hi[:, w, :], run_lo[:, c, 0:n], start=False, stop=True)
                    mm.then_inc(S["gate_mm"], 1)

            def cell_out(g, q):
                if q % (CB // QB) == 0:
                    pe.wait_ge(S["hidden_lo"], after("hidden_lo", (q * QB // CB, LAST), g))
                if in_graph_bank(g, q):
                    if q > 0:
                        pe.wait_ge(S["y_done"], after("y_done", q - 1, g))
                else:
                    if q == 0 or in_graph_bank(g, q - 1):
                        pe.wait_ge(S["gate_act"], after("gate_act", (CHAINS - 1, LAST, gates_of(LAST)[-1]), g))
                    if q >= GATE_BANKS and not in_graph_bank(g, q - GATE_BANKS):
                        pe.wait_ge(S["y_done"], after("y_done", q - GATE_BANKS, g))
                for b in range(QB):
                    o = turned_bank(g, q)[:, b * T:(b + 1) * T]
                    pe.matmul(o, state_hi[:, q * QB + b, :], ident16[:], start=True, stop=False)
                    mm = pe.matmul(o, state_lo[:, q * QB + b, :], ident16[:], start=False, stop=True)
                mm.then_inc(S["turned_mm"], 1)

            def free(sem, done, banks, key, g):
                last = bank_of(sem, banks, key, g)[1]
                if last is None:
                    pe.wait_ge(S["y_done"], after("y_done", NQ - 1, g))
                elif last >= 0 or not (isinstance(g, int) and g == 0):
                    pe.wait_ge(S[done], g * COUNT[done] + (last + 2))

            def mix_bank_free(key, g):
                free("mix_mm", "mix_evac", MIX_BANKS, key, g)

            def turn(g, q):
                if isinstance(g, int) and g == 0 and q == 0:
                    pe.wait_ge(wqkv_split, 2)
                pe.wait_ge(S["x1_done"], after("x1_done", q, g))
                mix_bank_free(("turn", q), g)
                for b in range(QB):
                    mm = pe.transpose(mix_bank(("turn", q), g)[:, b * T:(b + 1) * T], x1[:, q * QB + b, :], ident[:])
                mm.then_inc(S["mix_mm"], 1)

            def project(kind):
                def go(g, q):
                    pe.wait_ge(S["mix_evac"], after("mix_evac", ("turn", q), g))
                    mix_bank_free((kind, q), g)
                    c = slice(0, D) if kind == "query" else slice(D, 2 * D)
                    three(mix_bank((kind, q), g), wqkv_hi[:, c], wqkv_lo[:, c], x1t_hi[:, q % 2, :],
                          x1t_lo[:, q % 2, :]).then_inc(S["mix_mm"], 1)
                return go

            def project_value(g, q):
                pe.wait_ge(S["mix_evac"], after("mix_evac", ("turn", q), g))
                mix_bank_free(("value", q), g)
                c = slice(2 * D, 3 * D)
                for b in range(QB):
                    t = slice(b * T, (b + 1) * T)
                    mm = three(mix_bank(("value", q), g)[:, t], x1t_hi[:, q % 2, t], x1t_lo[:, q % 2, t],
                               wqkv_hi[:, c], wqkv_lo[:, c])
                mm.then_inc(S["mix_mm"], 1)

            def score(g, q, b):
                pe.wait_ge(stack_done[q // 2], (g * 2 + 2) * 16 * HEADS * SLOTS)
                free("score_mm", "max_done", 1, (q, b), g)
                bank = score_bank((q, b), g).rearrange("p (h t) -> p h t", h=HEADS)
                t = slice(b * T, (b + 1) * T)
                pe.matmul(bank, identb[:], mask[:, None, :].to_broadcast([P, HEADS, T]),
                          start=True, stop=False, skip_group_check=True)
                for h in range(HEADS):
                    mm = pe.matmul(bank[:, h, :], query_stack[0:SLOTS * HD, q // 2, q % 2, h, t],
                                   key_stack[0:SLOTS * HD, q // 2, q % 2, h, t],
                                   start=False, stop=h == HEADS - 1, skip_group_check=True)
                mm.then_inc(S["score_mm"], 1)

            def shift(g, q):
                pe.wait_ge(S["shift_lo"], after("shift_lo", q, g))
                mix_bank_free(("shift", q), g)
                pe.transpose(mix_bank(("shift", q), g).bitcast(F16)[0:2 * QB * HEADS, 0:P], shift_parts[:, q, :],
                             ident16[:]).then_inc(S["mix_mm"], 1)

            def expo(g, q, b):
                if isinstance(g, int) and g == 0:
                    pe.wait_ge(consts_done, CONSTS + 1)
                pe.wait_ge(shift_placed[q], g * 32 + 32)
                free("expo_mm", "expo_done", 1, (q, b), g)
                bank = expo_bank((q, b), g).rearrange("p (h t) -> p h t", h=HEADS)
                t = slice(b * T, (b + 1) * T)
                pe.matmul(bank, identb[:], mask_t[:, None, :].to_broadcast([P, HEADS, T]),
                          start=True, stop=False, skip_group_check=True)
                for h in range(HEADS):
                    mm = pe.matmul(bank[:, h, :], key_stack[0:STACK, q // 2, q % 2, h, t],
                                   query_stack[0:STACK, q // 2, q % 2, h, t],
                                   start=False, stop=h == HEADS - 1, skip_group_check=True)
                mm.then_inc(S["expo_mm"], 1)

            def mix(g, q, m):
                pe.wait_ge(S["prob_lo_done"], after("prob_lo_done", (q, 2 * m + 1), g))
                mix_bank_free((q, m), g)
                for b in range(2 * m, 2 * m + 2):
                    for h in range(HEADS):
                        at = ((b - 2 * m) * HEADS + h) * VW
                        o = mix_bank((q, m), g)[:, at:at + VW]
                        pe.matmul(o, prob_hi[:, b, h, :], value_hi[:, q, b, h, :], start=True, stop=False)
                        pe.matmul(o, prob_hi[:, b, h, :], value_lo[:, q, b, h, :], start=False, stop=False)
                        mm = pe.matmul(o, prob_lo[:, b, h, :], value_hi[:, q, b, h, :], start=False, stop=True)
                mm.then_inc(S["mix_mm"], 1)

            run(pe, {"weights": weights, "graph": graph, "cell_mm": cell_mm, "cell_out": cell_out, "turn": turn,
                     "query": project("query"), "key": project("key"), "value": project_value, "score": score,
                     "shift": shift, "expo": expo, "mix": mix})

        @block.scalar
        def _(act):
            owned(act, ["gate_act", "tanh_done", "hi_done", "expo_done"])
            def weights(g, n):
                act.wait_ge(weights_mm, n + 1)
                act.activation(w_hi[:, 4 * n:4 * n + 4, :],
                               ps_gate[:, n % GATE_BANKS, :].rearrange("p (c d) -> p c d", c=4),
                               ACT.Copy, scale=1.0 if n == 0 else 0.5).then_inc(weights_hi, 1)
                if n == WEIGHT_LOADS - 1:
                    act.wait_ge(small_in, 16 * SMALL)
                    act.activation(wqkv_hi[:], wqkv_sb[:], ACT.Copy).then_inc(wqkv_split, 1)

            def graph(g, q, k):
                src = graph_bank(q, g).rearrange("p (b t) -> p b t", b=QB)
                dst = (mixed_x[:, q % 2, :, :], h1[:, q % 2, :, :], mixed_h1[:, q % 2, :, :], quad(h2_hi, q))[k]
                act.wait_ge(S["graph_mm"], after("graph_mm", (q, k), g))
                act.activation(dst, src, ACT.Relu if k in (1, 3) else ACT.Copy).then_inc(S[f"graph_evac{q % 2}"], 1)
                if k == 0 and isinstance(g, int) and g == 0:
                    load_quad(1, q)

            def gates(g, c, s):
                p, n = STEPS[s][0], size(s)
                for i in gates_of(s):
                    if s == 0 and not (isinstance(g, int) and g == 0) and i == I_:
                        act.wait_ge(S["hidden_lo"], after("hidden_lo", (c, LAST), g - 1))
                    elif 0 < s < CB // QB and i == I_:
                        act.wait_ge(S["hidden_lo"], after("hidden_lo", (c, s - 1), g))
                    act.wait_ge(S["gate_mm"], after("gate_mm", (c, s, i), g))
                    w = (p - 1) * 4 + i
                    bc, scale = (bias, 1.0) if i == G_ else (bias_half, 0.5)
                    act.activation(gate[:, c, i, 0:n], gate_bank(g, c, s, i), ACT.Tanh, bias=bc[:, w:w + 1],
                                   scale=scale).then_inc(S["gate_act"], 1)

            def cell_tanh(g, c, s):
                n = size(s)
                done = "input_done" if STEPS[s][1] == 0 else "cell_done"
                act.wait_ge(S[done], after(done, (c, s), g))
                act.activation(tanh_c[:, c, 0:n], cell[:, c, 0:n], ACT.Tanh, scale=0.5).then_inc(S["tanh_done"], 1)

            def high(kind):
                def go(g, q):
                    dst = x1t_hi[:, q % 2, :] if kind == "turn" else part[kind, "hi"][:, q, :]
                    act.wait_ge(S["mix_mm"], after("mix_mm", (kind, q), g))
                    act.activation(dst, mix_bank((kind, q), g), ACT.Copy).then_inc(S["hi_done"], 1)
                return go

            def value_high(g, q):
                act.wait_ge(S["mix_mm"], after("mix_mm", ("value", q), g))
                act.activation(value_hi[:, q, :, :, 0:HD],
                               mix_bank(("value", q), g).rearrange("p (b h d) -> p b h d", b=QB, h=HEADS),
                               ACT.Copy).then_inc(S["hi_done"], 1)

            def expo(g, q, b):
                act.wait_ge(S["expo_mm"], after("expo_mm", (q, b), g))
                act.activation(prob_t[:, b, :, :], expo_bank((q, b), g).rearrange("p (h t) -> p h t", h=HEADS), ACT.Exp,
                               scale=HD ** -0.5).then_inc(S["expo_done"], 1)

            def load_quad(g, q):
                if not isinstance(g, int) or g > 0:
                    act.wait_ge(S["graph_mm"], after("graph_mm", (q, 0), g - 1))
                act.dma_start(x_in[:, q, :, :], x_quads[g, q]).then_inc(x_in_done[q], 16)

            def load(g):
                for q in range(NQ):
                    load_quad(g, q)

            run(act, {"load": load, "weights": weights, "graph": graph, "cell_mm": gates, "cell_tanh": cell_tanh,
                      "turn": high("turn"), "query": high("query"), "key": high("key"), "value": value_high,
                      "expo": expo})

        @block.vector
        def _(dve):
            owned(dve, ["graph_evac0", "graph_evac1", "input_done", "forget_done", "cell_done",
                        "hidden_done", "hidden_hi", "hidden_lo", "y_done", "stats_done1", "stats_done2",
                        "x1_done", "out_done", "mix_evac", "max_done", "shift_hi", "shift_lo",
                        "recip_done"])
            dve.wait_ge(small_in, 16 * SMALL)
            dve.tensor_tensor(b_sum[:], b_raw[:, 0, :], b_raw[:, 1, :], ALU.add).then_inc(prep_dve, 1)
            dve.wait_ge(prep_mm, 1)
            dve.tensor_copy(adj_t[:], ps_score[:, 0, :]).then_inc(prep_dve, 1)
            dve.wait_ge(prep_mm, 3)
            dve.tensor_copy(rows[:, 0, :], ps_mix[0:1, 0, 0:T]).then_inc(prep_dve, 1)
            dve.wait_ge(prep_dve, 3)
            dve.tensor_copy(rows_part[:, 0, :, :], rows).then_inc(prep_dve, 1)
            dve.wait_ge(prep_dve, 4)
            dve.tensor_tensor(rows_left, rows, rows_part[:, 0, :, :], ALU.subtract).then_inc(rows_done, 1)
            dve.wait_ge(rows_done, 1)
            dve.tensor_copy(rows_part[:, 1, :, :], rows_left).then_inc(prep_dve, 1)
            dve.wait_ge(prep_dve, 5)
            dve.tensor_tensor(rows_part[:, 2, :, :], rows_left, rows_part[:, 1, :, :],
                              ALU.subtract).then_inc(prep_dve, 1)
            dve.tensor_scalar(mask[:], adj_sb[:], 0.0, MASKED, ALU.is_equal, ALU.mult).then_inc(prep_dve, 1)
            dve.tensor_scalar(mask_t[:], ps_score[:, 0, :], 0.0, MASKED, ALU.is_equal,
                              ALU.mult).then_inc(prep_dve, 1)
            dve.tensor_copy(bias[:], ps_expo[:, 0, 0:NW]).then_inc(prep_dve, 1)
            dve.tensor_scalar(bias_half[:], ps_expo[:, 0, 0:NW], 0.5, None, ALU.mult).then_inc(prep_dve, 1)
            dve.wait_ge(prep_mm, 4)
            dve.tensor_copy(bias_rows[:].rearrange("p a d -> p (a d)"), ps_mix[0:9, 1, 0:3 * D]).then_inc(prep_dve, 1)

            def weights(g, n):
                dve.wait_ge(weights_hi, n + 1)
                dve.scalar_tensor_tensor(out=w_lo[:, 4 * n:4 * n + 4, :],
                                         in0=ps_gate[:, n % GATE_BANKS, :].rearrange("p (c d) -> p c d", c=4),
                                         scalar=1.0 if n == 0 else 0.5, in1=w_hi[:, 4 * n:4 * n + 4, :],
                                         op0=ALU.mult, op1=ALU.subtract).then_inc(split_done, 1)
                if n == WEIGHT_LOADS - 1:
                    dve.wait_ge(wqkv_split, 1)
                    dve.tensor_tensor(wqkv_lo[:], wqkv_sb[:], wqkv_hi[:], ALU.subtract).then_inc(wqkv_split, 1)

            def graph(g, q, k):
                src = graph_bank(q, g).rearrange("p (b t) -> p b t", b=QB)
                if k == 3:
                    dve.wait_ge(S[f"graph_evac{q % 2}"], after(f"graph_evac{q % 2}", (q, "hi"), g))
                    dve.scalar_tensor_tensor(out=quad(h2_lo, q), in0=src, scalar=0.0, in1=quad(h2_hi, q),
                                             op0=ALU.max, op1=ALU.subtract).then_inc(S[f"graph_evac{q % 2}"], 1)

            def new_cell(g, c, s):
                n = size(s)
                late = STEPS[s][1] > 0
                dve.wait_ge(S["gate_act"], after("gate_act", (c, s, G_), g))
                dve.scalar_tensor_tensor(out=(inp if late else cell)[:, c, 0:n], in0=gate[:, c, I_, 0:n], scalar=1.0,
                                         in1=gate[:, c, G_, 0:n], op0=ALU.add,
                                         op1=ALU.mult).then_inc(S["input_done"], 1)
                if late:
                    dve.wait_ge(S["gate_act"], after("gate_act", (c, s, F_), g))
                    dve.scalar_tensor_tensor(out=forget[:, c, 0:n], in0=gate[:, c, F_, 0:n], scalar=1.0,
                                             in1=cell[:, c, 0:n], op0=ALU.add,
                                             op1=ALU.mult).then_inc(S["forget_done"], 1)
                    dve.wait_ge(S["forget_done"], after("forget_done", (c, s), g))
                    dve.scalar_tensor_tensor(out=cell[:, c, 0:n], in0=forget[:, c, 0:n], scalar=0.5,
                                             in1=inp[:, c, 0:n], op0=ALU.mult,
                                             op1=ALU.add).then_inc(S["cell_done"], 1)

            def cell_end(g, c, s):
                n = size(s)
                dve.wait_ge(S["tanh_done"], after("tanh_done", (c, s), g))
                dve.scalar_tensor_tensor(out=hidden[:, c, 0:n], in0=gate[:, c, O_, 0:n], scalar=1.0,
                                         in1=tanh_c[:, c, 0:n], op0=ALU.add,
                                         op1=ALU.mult).then_inc(S["hidden_done"], 1)
                ends = ends_window(s)
                hi = columns(state_hi, c, s) if ends else dense(run_hi[:, c, :], s)
                lo = columns(state_lo, c, s) if ends else dense(run_lo[:, c, :], s)
                dve.wait_ge(S["hidden_done"], after("hidden_done", (c, s), g))
                dve.tensor_copy(hi, dense(hidden[:, c, :], s)).then_inc(S["hidden_hi"], 1)
                dve.wait_ge(S["hidden_hi"], after("hidden_hi", (c, s), g))
                dve.tensor_tensor(lo, dense(hidden[:, c, :], s), hi, ALU.subtract).then_inc(S["hidden_lo"], 1)

            def cell_out(g, q):
                dve.wait_ge(x_res_done[q], g * 16 + 16)
                dve.wait_ge(S["turned_mm"], after("turned_mm", q, g))
                dve.scalar_tensor_tensor(out=quad(y, q), in0=turned_bank(g, q).rearrange("p (b d) -> p b d", b=QB),
                                         scalar=0.5, in1=quad(y, q), op0=ALU.mult,
                                         op1=ALU.add).then_inc(S["y_done"], 1)

            def moments_of(n):
                def go(g, q):
                    i = int(n) - 1
                    src, at = (y, q) if n == "1" else (z, q % 2)
                    if n == "1":
                        dve.wait_ge(S["y_done"], after("y_done", q, g))
                    else:
                        dve.wait_ge(S["z_done"], after("z_done", (q, 1), g))
                    for b in range(QB):
                        ins = dve.bn_stats(stats[:, i, q * QB + b, :], src[:, at * QB + b, :])
                    ins.then_inc(S["stats_done" + n], 1)
                return go

            def normalise(n):
                def go(g, q):
                    i = int(n) - 1
                    src, dst, at, done = (y, x1, q, "x1_done") if n == "1" else (z, result, q % 2, "out_done")
                    dve.wait_ge(S["rstd_done" + n], after("rstd_done" + n, q, g))
                    if n == "2":
                        dve.wait_ge(out_stored[q % 2], (g * (NQ // 2) + q // 2 + 1) * 16)
                    elif not (isinstance(g, int) and g == 0):
                        dve.wait_ge(S["z_done"], before("z_done", order_of("z_done", g)[0], g))
                    for b in range(QB):
                        r = q * QB + b
                        ins = dve.tensor_scalar(dst[:, at * QB + b, :], src[:, at * QB + b, :], mean[:, i, r:r + 1],
                                                rstd[:, i, r:r + 1], ALU.subtract, ALU.mult)
                    ins.then_inc(S[done], 1)
                return go

            def low(kind):
                def go(g, q):
                    hi, lo = ((x1t_hi[:, q % 2, :], x1t_lo[:, q % 2, :]) if kind == "turn"
                              else (part[kind, "hi"][:, q, :], part[kind, "lo"][:, q, :]))
                    dve.wait_ge(S["hi_done"], after("hi_done", (kind, q), g))
                    dve.tensor_tensor(lo, mix_bank((kind, q), g), hi, ALU.subtract).then_inc(S["mix_evac"], 1)
                return go

            def value_low(g, q):
                dve.wait_ge(S["hi_done"], after("hi_done", ("value", q), g))
                dve.tensor_tensor(value_lo[:, q, :, :, 0:HD],
                                  mix_bank(("value", q), g).rearrange("p (b h d) -> p b h d", b=QB, h=HEADS),
                                  value_hi[:, q, :, :, 0:HD], ALU.subtract).then_inc(S["mix_evac"], 1)

            def row_maxima(g, q, b):
                dve.wait_ge(S["score_mm"], after("score_mm", (q, b), g))
                dve.tensor_reduce(row_max[:, q, b:QB * HEADS:QB],
                                  score_bank((q, b), g).rearrange("p (h t) -> p h t", h=HEADS), AX_X,
                                  ALU.max).then_inc(S["max_done"], 1)

            def parts(g, q):
                n = QB * HEADS
                dve.wait_ge(S["max_done"], after("max_done", (q, QB - 1), g))
                dve.tensor_scalar(shift_parts[:, q, 0:n], row_max[:, q, :], -1.0 / SHIFT_UNIT, None,
                                  ALU.mult).then_inc(S["shift_hi"], 1)
                dve.wait_ge(S["shift_hi"], after("shift_hi", q, g))
                dve.scalar_tensor_tensor(out=shift_parts[:, q, n:2 * n], in0=row_max[:, q, :], scalar=-1.0 / SHIFT_UNIT,
                                         in1=shift_parts[:, q, 0:n], op0=ALU.mult,
                                         op1=ALU.subtract).then_inc(S["shift_lo"], 1)

            def shift(g, q):
                n = QB * HEADS
                dve.wait_ge(S["mix_mm"], after("mix_mm", ("shift", q), g))
                dve.tensor_copy(shift_t[:, q, :],
                                mix_bank(("shift", q), g).bitcast(F16)[0:2 * n, 0:P]).then_inc(S["mix_evac"], 1)

            def mix(g, q, m):
                heads = mix_bank((q, m), g)[:, 0:2 * HEADS * VW].rearrange("p (n v) -> p n v", v=VW)
                dve.wait_ge(S["mix_mm"], after("mix_mm", (q, m), g))
                dve.reciprocal(recip[:, m, :], heads[:, :, HD]).then_inc(S["recip_done"], 1)
                dve.wait_ge(S["recip_done"], after("recip_done", (q, m), g))
                dve.wait_ge(S["z_done"], before("z_done", (q, m), g))
                dve.tensor_tensor(mixed[:, m, :, :], heads[:, :, 0:HD],
                                  recip[:, m, :, None].to_broadcast([P, 2 * HEADS, HD]),
                                  ALU.mult).then_inc(S["mix_evac"], 1)

            run(dve, {"weights": weights, "graph": graph, "cell_mm": new_cell, "cell_end": cell_end,
                      "cell_out": cell_out, "stat1": moments_of("1"), "norm1": normalise("1"),
                      "turn": low("turn"), "query": low("query"), "key": low("key"), "value": value_low,
                      "score": row_maxima, "parts": parts, "shift": shift, "mix": mix,
                      "stat2": moments_of("2"), "out": normalise("2")})


INPUTS = ["x", "adj", "L0_gnn_Wg0", "L0_gnn_bg0", "L0_gnn_Wg1", "L0_gnn_bg1", "L0_gnn_Wih", "L0_gnn_Whh",
          "L0_gnn_bih", "L0_gnn_bhh", "L1_gnn_W"]


def kernel(**inputs):
    import concourse.bacc as bacc
    from concourse.bass_utils import run_bass_kernel_spmd

    nc = bacc.Bacc("TRN2", target_bir_lowering=False, num_devices=1)
    arrays, args = {}, []
    for name in INPUTS:
        a = np.ascontiguousarray(inputs[name])
        arrays[f"in_{name}"] = a
        args.append(nc.dram_tensor(f"in_{name}", a.shape, mybir.dt.from_np(a.dtype), kind="ExternalInput").ap())
    args.append(nc.dram_tensor("out_0", (B, T, D), F32, kind="ExternalOutput").ap())
    build(nc, *args)
    r = run_bass_kernel_spmd(nc, [arrays], core_ids=[0])
    return r.results[0]["out_0"]
```
